# Optimizing a Trainium2 kernel written in Bass

```python
import numpy as np
import jax
import jax.numpy as jnp

def _softmax(x, axis=-1):
    return jax.nn.softmax(x, axis=axis)
def _gelu(x):
    return jax.nn.gelu(x, approximate=True)
def _silu(x):
    return jax.nn.silu(x)
def _sigmoid(x):
    return jax.nn.sigmoid(x)
def _layernorm(x, axis=-1, eps=1e-5):
    m = jnp.mean(x, axis=axis, keepdims=True)
    v = jnp.var(x, axis=axis, keepdims=True)
    return (x - m) / jnp.sqrt(v + eps)
def _scatter_add(tgt, idx, src, axis=0):
    return tgt.at[idx].add(src)
def _segment_sum(src, seg, n):
    return jax.ops.segment_sum(src, seg, n)

kernel_name = 'mk_conv_preact_d2_conv_nchw256_d11418'

def setup_inputs(seed: int = 0):
    np.random.seed(seed)
    _w = jnp.asarray
    def _rec_inputs():
        import jax
        import jax.numpy as jnp
        _gk = jax.random.key(seed)
        x = -7.109e-05 + 0.9999 * jax.random.normal(jax.random.fold_in(_gk, 1), (16, 256, 128, 128), jnp.float32)
        return x
    x = _rec_inputs()
    def _L0_conv_setup():
        import jax, jax.numpy as jnp
        import numpy as np
        EPS = 1e-05

        def instance_norm(x):
            mean = jnp.mean(x, axis=(2, 3), keepdims=True)
            var = jnp.var(x, axis=(2, 3), keepdims=True)
            return (x - mean) * jax.lax.rsqrt(var + EPS)

        def conv1x1(x, w, b):
            return jnp.einsum('bchw,oc->bohw', x, w) + b[None, :, None, None]
        key = jax.random.key(seed)
        k1, k2, k3 = jax.random.split(key, 3)
        B, Cin, Cout, H, W = (16, 256, 256, 128, 128)
        x = jax.random.normal(k1, (B, Cin, H, W), dtype=jnp.float32)
        s1 = 1.0 / np.sqrt(Cin)
        w1 = jax.random.uniform(k2, (Cout, Cin), jnp.float32, -s1, s1)
        b1 = jax.random.uniform(jax.random.fold_in(k2, 1), (Cout,), jnp.float32, -s1, s1)
        s2 = 1.0 / np.sqrt(Cout)
        w2 = jax.random.uniform(k3, (Cout, Cout), jnp.float32, -s2, s2)
        b2 = jax.random.uniform(jax.random.fold_in(k3, 1), (Cout,), jnp.float32, -s2, s2)
        return {'x': x, 'w1': w1, 'b1': b1, 'w2': w2, 'b2': b2}
    _L0_conv_all = _L0_conv_setup()
    _L0_conv_in = {k: v for k, v in _L0_conv_all.items() if k in ('w1', 'b1', 'w2', 'b2', )}
    del _L0_conv_all

    def _L1_conv_setup():
        import jax, jax.numpy as jnp
        import numpy as np
        EPS = 1e-05
        SLOPE = 0.01
        C = 256
        key = jax.random.key(seed)
        k = jax.random.split(key, 5)
        B, H, W = (8, 128, 128)
        x = jax.random.normal(k[0], (B, C, H, W), dtype=jnp.float32)
        attn_w1 = jax.random.normal(k[1], (C // 4, C), dtype=jnp.float32) * (1.0 / np.sqrt(C))
        attn_w2 = jax.random.normal(k[2], (C, C // 4), dtype=jnp.float32) * (1.0 / np.sqrt(C // 4))
        refine_w = jax.random.normal(k[3], (C, 1, 3, 3), dtype=jnp.float32) * (1.0 / 3.0)
        refine_b = jax.random.normal(k[4], (C,), dtype=jnp.float32) * 0.01
        return {'x': x, 'attn_w1': attn_w1, 'attn_w2': attn_w2, 'refine_w': refine_w, 'refine_b': refine_b}
    _L1_conv_all = _L1_conv_setup()
    _L1_conv_in = {k: v for k, v in _L1_conv_all.items() if k in ('attn_w1', 'attn_w2', 'refine_w', 'refine_b', )}
    del _L1_conv_all

    return {
        "x": x,
        "L0_conv_w1": _L0_conv_in["w1"],
        "L0_conv_b1": _L0_conv_in["b1"],
        "L0_conv_w2": _L0_conv_in["w2"],
        "L0_conv_b2": _L0_conv_in["b2"],
        "L1_conv_attn_w1": _L1_conv_in["attn_w1"],
        "L1_conv_attn_w2": _L1_conv_in["attn_w2"],
        "L1_conv_refine_w": _L1_conv_in["refine_w"],
        "L1_conv_refine_b": _L1_conv_in["refine_b"],
    }

def reference(x, L0_conv_w1, L0_conv_b1, L0_conv_w2, L0_conv_b2, L1_conv_attn_w1, L1_conv_attn_w2, L1_conv_refine_w, L1_conv_refine_b):
    import jax
    import jax.numpy as jnp
    def _L0_conv_ref(x, w1, b1, w2, b2):
        import jax, jax.numpy as jnp
        import numpy as np
        EPS = 1e-05

        def instance_norm(x):
            mean = jnp.mean(x, axis=(2, 3), keepdims=True)
            var = jnp.var(x, axis=(2, 3), keepdims=True)
            return (x - mean) * jax.lax.rsqrt(var + EPS)

        def conv1x1(x, w, b):
            return jnp.einsum('bchw,oc->bohw', x, w) + b[None, :, None, None]
        h = jax.nn.relu(conv1x1(instance_norm(x), w1, b1))
        out = jax.nn.relu(conv1x1(instance_norm(h), w2, b2))
        return out

    def _L1_conv_ref(x, attn_w1, attn_w2, refine_w, refine_b):
        import jax, jax.numpy as jnp
        import numpy as np
        EPS = 1e-05
        SLOPE = 0.01
        C = 256
        xw = jax.lax.stop_gradient(x)
        p = jnp.mean(xw, axis=(2, 3))
        h = jax.nn.leaky_relu(p @ attn_w1.T, SLOPE)
        a = jax.nn.sigmoid(h @ attn_w2.T)
        y = xw * a[:, :, None, None]
        y = jax.lax.conv_general_dilated(y, refine_w, window_strides=(1, 1), padding='SAME', feature_group_count=C, dimension_numbers=('NCHW', 'OIHW', 'NCHW'))
        y = y + refine_b[None, :, None, None]
        mu = jnp.mean(y, axis=(2, 3), keepdims=True)
        var = jnp.mean(jnp.square(y - mu), axis=(2, 3), keepdims=True)
        y = (y - mu) * jax.lax.rsqrt(var + EPS)
        return jax.nn.leaky_relu(y, SLOPE)

    def _gn(v, G=32, eps=1e-5):
        B_, C_, H_, W_ = v.shape
        g = v.reshape(B_, G, C_ // G, H_, W_)
        m = jnp.mean(g, axis=(2, 3, 4), keepdims=True)
        s = jnp.var(g, axis=(2, 3, 4), keepdims=True)
        return ((g - m) / jnp.sqrt(s + eps)).reshape(v.shape)

    def _ln_c(v, eps=1e-6):
        m = jnp.mean(v, axis=1, keepdims=True)
        s = jnp.var(v, axis=1, keepdims=True)
        return (v - m) / jnp.sqrt(s + eps)

    def _ln_t(v, eps=1e-5):
        m = jnp.mean(v, axis=-1, keepdims=True)
        s = jnp.var(v, axis=-1, keepdims=True)
        return (v - m) / jnp.sqrt(s + eps)

    def _to_tokens(v):
        B_, C_, H_, W_ = v.shape
        return v.reshape(B_, C_, H_ * W_).transpose(0, 2, 1)
    def _from_tokens(t, like):
        B_, C_, H_, W_ = like.shape
        return t.transpose(0, 2, 1).reshape(B_, C_, H_, W_)

    x = x + _L0_conv_ref(_gn(x), L0_conv_w1, L0_conv_b1, L0_conv_w2, L0_conv_b2)
    x = x + _L1_conv_ref(_gn(x), L1_conv_attn_w1, L1_conv_attn_w2, L1_conv_refine_w, L1_conv_refine_b)
    return x


_drawn_inputs = setup_inputs


def setup_inputs(seed=0):
    import zlib

    import numpy as np

    out = dict(_drawn_inputs(seed))
    spreads = {}
    factors = {'L0_conv_b1': 4.175,
     'L0_conv_b2': 2.676,
     'L1_conv_attn_w1': 23.093,
     'L1_conv_attn_w2': 64.0,
     'L1_conv_refine_b': 64.0}
    for name, (base, spread) in spreads.items():
        noise = np.random.default_rng([zlib.crc32(name.encode()), seed]).standard_normal(out[name].shape)
        drawn = base * np.exp(spread * noise) if base else spread * noise
        out[name] = jnp.asarray(drawn.astype(out[name].dtype))
    for name, factor in factors.items():
        out[name] = (out[name] * factor).astype(out[name].dtype)
    return out
```

```python
from contextlib import ExitStack

import concourse.bass as bass
from concourse import mybir

ALU = mybir.AluOpType
ACT = mybir.ActivationFunctionType
F32 = mybir.dt.float32
AX_X = mybir.AxisListType.X

P = 128
EPS = 1e-5
SLOPE = 0.01
TAPS = [(dy, dx) for dy in (-1, 0, 1) for dx in (-1, 0, 1)]
PE_TAPS = [[4, 1, 7], [4, 1, 7]]
DVE_TAPS = [[t for t in range(9) if t not in PE_TAPS[o]] for o in range(2)]


def conv_preact_kernel(nc, x, w1t, b1, w2t, b2, a1t, a2t, rw, rb, out):
    B, C, H, W = x.shape
    HALVES = C // P
    HID = a1t.shape[1]
    GROUP = C // 32
    ROWS = 8
    CP = ROWS * W
    K = H // ROWS
    BANK = 512
    BROWS = BANK // W
    NPIX = H * W
    PITCH = W + 2
    NT = [len(DVE_TAPS[o]) for o in range(HALVES)]
    assert HALVES == 2 and CP == 2 * BANK and K % 2 == 0

    xv = x.rearrange("b (o p) h w -> p (b o) (h w)", p=P)
    ov = out.rearrange("b (o p) h w -> p (b o) (h w)", p=P)
    x1_dram = nc.dram_tensor("x1_dram", [B, C, NPIX], F32, kind="Internal").ap()
    x1v = x1_dram.rearrange("b (o p) n -> p (b o) n", p=P)

    with ExitStack() as ctx:
        def sb(name, shape):
            return ctx.enter_context(nc.sbuf_tensor(name, shape, F32))

        def sem(name):
            return ctx.enter_context(nc.semaphore(name))

        body = sb("body", [P, HALVES, H + 2, PITCH])
        x_ring = sb("x_ring", [P, 2, HALVES, CP])
        stat_ring = sb("stat_ring", [P, 2, HALVES, CP])
        fin_ring = sb("fin_ring", [P, 2, HALVES, CP])
        unused = ctx.enter_context(nc.sbuf_tensor("unused", [P, 4, CP], mybir.dt.bfloat16))
        w1_raw = sb("w1_raw", [P, HALVES, C])
        w2_raw = sb("w2_raw", [P, HALVES, C])
        w1_s = sb("w1_s", [P, HALVES, C])
        w2_s = sb("w2_s", [P, HALVES, C])
        att1 = sb("att1", [P, HALVES, HID])
        att2 = sb("att2", [HID, C])
        taps = sb("taps", [P, HALVES, 9])
        vecs = sb("vecs", [P, 3, HALVES])
        b1c, b2c, rbc = (vecs[:, i, :] for i in range(3))
        ident = sb("ident", [P, P])
        group = sb("group", [P, P])
        diag = sb("diag", [P, HALVES, max(map(len, PE_TAPS)), P])
        minus_half = sb("minus_half", [P, 4])
        tap_sum = sb("tap_sum", [P, HALVES])
        edge_rows = sb("edge_rows", [P, HALVES, 2])
        edge_cols = sb("edge_cols", [P, HALVES, 2])
        part = sb("part", [P, 8, K])
        total = sb("total", [P, 8])
        u_part = sb("u_part", [P, 4, K + 2])
        u_total = sb("u_total", [P, 4])
        h_stats = sb("h_stats", [P, HALVES, 2 * K, 6])
        h_mv = sb("h_mv", [P, HALVES, 2])
        h_ve = sb("h_ve", [P, HALVES])
        h_rstd = sb("h_rstd", [P, HALVES])
        beta2 = sb("beta2", [P, HALVES])
        neg_beta2 = sb("neg_beta2", [P, HALVES])
        bias1 = sb("bias1", [P, HALVES])
        neg_pivot = sb("neg_pivot", [P, 4])
        add_back = sb("add_back", [P, 4])
        dm = sb("dm", [P, 4])
        var = sb("var", [P, 4])
        mean = sb("mean", [P, 4])
        gmean = sb("gmean", [P, 4])
        dev = sb("dev", [P, 4])
        tmp4 = sb("tmp4", [P, 4])
        grstd = sb("grstd", [P, 4])
        xs_ = sb("xs_", [P, HALVES])
        xr = sb("xr", [P, HALVES])
        pooled = sb("pooled", [P, HALVES])
        hidden_raw = sb("hidden_raw", [HID, 1])
        hidden = sb("hidden", [HID, 1])
        attn = sb("attn", [P, HALVES])
        alpha = sb("alpha", [P, HALVES])
        padk = sb("padk", [P, HALVES])
        u_neg_pivot = sb("u_neg_pivot", [P, HALVES])
        k_rows = sb("k_rows", [P, HALVES, 2])
        k_cols = sb("k_cols", [P, HALVES, 2])
        k_corner = sb("k_corner", [P, HALVES, 2, 2])
        uv = sb("uv", [P, 8, HALVES])
        u_scale = sb("u_scale", [P, HALVES])
        u_shift = sb("u_shift", [P, HALVES])
        relu_scale = sb("relu_scale", [P, HALVES])
        relu_shift = sb("relu_shift", [P, HALVES])
        slope_scale = sb("slope_scale", [P, HALVES])
        out_shift = sb("out_shift", [P, HALVES])

        ps_conv = ctx.enter_context(nc.psum_tensor("ps_conv", [P, HALVES, CP], F32))
        ps_dw = ctx.enter_context(nc.psum_tensor("ps_dw", [P, HALVES, CP], F32))
        ps_gm, ps_gq = ps_conv[:, 0, 0:4], ps_conv[:, 0, 4:8]
        ps_b1, ps_at = ps_conv[:, 0, 8:10], ps_conv[:, 0, 10:12]
        ps_hid = ps_conv[0:HID, 0, 12:13]
        ps_b2 = ps_dw[:, 1, 0:2]

        const_loaded = sem("const_loaded")
        const_pool = sem("const_pool")
        const_dve = sem("const_dve")
        x_loaded = [sem(f"x_loaded{q}") for q in range(2)]
        stat_loaded = [sem(f"stat_loaded{q}") for q in range(2)]
        fin_loaded = [sem(f"fin_loaded{n}") for n in range(4)]
        out_stored = [sem(f"out_stored{n}") for n in range(4)]
        spilled = [sem(f"spilled{q}") for q in range(2)]
        conv1_done = sem("conv1_done")
        h_written = sem("h_written")
        conv2_done = sem("conv2_done")
        x1_half = sem("x1_half")
        x1_squared = sem("x1_squared")
        dw_products = sem("dw_products")
        tap_added = sem("tap_added")
        u_written = sem("u_written")
        u_summed = sem("u_summed")
        x_pivot = sem("x_pivot")
        x_summed = sem("x_summed")
        relu_done = sem("relu_done")
        leaky_done = sem("leaky_done")
        out_ready = sem("out_ready")
        h_counted = sem("h_counted")
        h_chain = sem("h_chain")
        g_chain = sem("g_chain")
        x_chain = sem("x_chain")
        a_chain = sem("a_chain")
        u_chain = sem("u_chain")
        edge_summed = sem("edge_summed")

        H_STEPS = ["top", "aggr0", "aggr1", "ve", "rstd", "w0", "w1", "prod", "neg", "beta"]
        G_STEPS = ["total", "dm", "dm2", "var", "var0", "mean", "prod", "gmean", "dev", "dev2",
                   "q", "prod2", "ve", "rstd"]
        X_STEPS = ["t", "t2", "te", "rstd", "s", "w0", "w1", "prod", "bias", "pivots", "upivot"]
        A_STEPS = ["pool", "hid", "copy", "leaky", "att", "sigmoid", "alpha", "k", "krows", "kcols",
                   "kcorner"]
        U_STEPS = ["rows", "cols", "corner", "total", "m", "m2", "var", "var0", "mean", "t", "t2",
                   "te", "rstd", "scale", "kw", "akw", "c0", "am", "mu", "d", "shift", "scale99",
                   "shift99", "scale01", "last"]

        CONST_CLEARED = 4
        CONST_DVE = CONST_CLEARED + sum(map(len, PE_TAPS)) + 3

        def after(steps, n, name):
            return n * len(steps) + steps.index(name) + 1

        def rows(o, first, count, c0=1, cn=W):
            return body[:, o, bass.ds(first, count), c0:c0 + cn]

        def grid(ap):
            return ap.rearrange("p (r w) -> p r w", w=W)

        block = ctx.enter_context(nc.Block())

        @block.sync
        def _(sp):
            for dst, src in ((w1_raw[:], w1t.rearrange("(o p) n -> p o n", p=P)),
                             (w2_raw[:], w2t.rearrange("(o p) n -> p o n", p=P)),
                             (att1[:], a1t.rearrange("(o p) n -> p o n", p=P)),
                             (att2[:], a2t),
                             (taps[:], rw.rearrange("(o p) t -> p o t", p=P)),
                             (b1c, b1), (b2c, b2), (rbc, rb)):
                sp.dma_start(dst, src).then_inc(const_loaded, 16)

            def load_x(b, k, q):
                sp.dma_start(x_ring[:, q], xv[:, bass.ds(b * HALVES, HALVES), bass.ds(k * CP, CP)]
                             ).then_inc(x_loaded[q], 16)

            def load_fin(b, k, q):
                for o in range(HALVES):
                    sp.dma_start(fin_ring[:, q, o:o + 1],
                                 x1v[:, bass.ds(b * HALVES + o, 1), bass.ds(k * CP, CP)]
                                 ).then_inc(fin_loaded[2 * q + o], 16)

            def reload_fin(b, k, j, q):
                for o in range(HALVES):
                    sp.wait_ge(out_stored[2 * q + o], 16 * (b * (K // 2) + j))
                load_fin(b, k, q)

            def conv1_streams(b, final):
                with sp.Fori(1, K // 2) as j:
                    for q in range(2):
                        k = 2 * j + q
                        sp.wait_ge(conv1_done, b * 2 * K + 2 * (k - 1))
                        load_x(b, k, q)
                        if final:
                            reload_fin(b - 1, k, j, q)
                for q in range(2):
                    sp.wait_ge(conv1_done, b * 2 * K + 2 * (K - 1 + q))
                    load_x(b, q, q)

            def spill_x1(b, k, q):
                sp.wait_ge(x1_half, b * 2 * K + 2 * (k + 1))
                for o in range(HALVES):
                    sp.dma_start(x1v[:, bass.ds(b * HALVES + o, 1), bass.ds(k * CP, CP)]
                                 .rearrange("p a (r w) -> p (a r) w", w=W),
                                 rows(o, k * ROWS + 1, ROWS)).then_inc(spilled[q], 16)

            def conv2_streams(b, last):
                with sp.Fori(0, K // 2 - 1) as j:
                    for q in range(2):
                        k = 2 * j + q
                        spill_x1(b, k, q)
                        load_x(b, k + 2, q)
                for q in range(2):
                    spill_x1(b, K - 2 + q, q)
                    if not last:
                        load_x(b + 1, q, q)
                for q in range(2):
                    sp.wait_ge(spilled[q], 32 * (b + 1) * (K // 2))
                    for o in range(HALVES):
                        if not (isinstance(b, int) and b == 0):
                            sp.wait_ge(out_stored[2 * q + o], 16 * b * (K // 2))
                    load_fin(b, q, q)

            for q in range(2):
                load_x(0, q, q)
            conv1_streams(0, False)
            conv2_streams(0, False)
            with sp.Fori(1, B - 1) as b:
                conv1_streams(b, True)
                conv2_streams(b, False)
            conv1_streams(B - 1, True)
            conv2_streams(B - 1, True)
            with sp.Fori(1, K // 2) as j:
                for q in range(2):
                    reload_fin(B - 1, 2 * j + q, j, q)

        @block.gpsimd
        def _(pool):
            nc.gpsimd.memset(ident[:], 0.0).then_inc(const_pool, 1)
            nc.gpsimd.memset(group[:], 1.0 / GROUP).then_inc(const_pool, 1)
            nc.gpsimd.memset(minus_half[:], -0.5).then_inc(const_pool, 1)
            pool.wait_ge(const_pool, 3)
            nc.gpsimd.affine_select(out=ident[:], in_=ident[:], compare_op=ALU.not_equal, fill=1.0,
                                    base=0, pattern=[[-1, P]], channel_multiplier=1
                                    ).then_inc(const_pool, 1)
            blocks = group[:].rearrange("p (g c) -> p g c", c=GROUP)
            nc.gpsimd.affine_select(out=blocks, in_=blocks, compare_op=ALU.is_ge, fill=0.0, base=0,
                                    pattern=[[-GROUP, P // GROUP], [0, GROUP]], channel_multiplier=1
                                    ).then_inc(const_pool, 1)
            pool.wait_ge(const_pool, 5)
            nc.gpsimd.affine_select(out=blocks, in_=blocks, compare_op=ALU.is_ge, fill=0.0,
                                    base=GROUP - 1, pattern=[[GROUP, P // GROUP], [0, GROUP]],
                                    channel_multiplier=-1).then_inc(const_pool, 1)

            def power(out_, in_, n):
                return nc.gpsimd.tensor_tensor(out_, in_, minus_half[:, 0:n], ALU.pow)

            def group_rsqrts(n, with_x):
                pool.wait_ge(g_chain, after(G_STEPS, n, "ve"))
                power(grstd[:], tmp4[:], 4).then_inc(g_chain, 1)
                if with_x:
                    pool.wait_ge(x_chain, after(X_STEPS, n, "te"))
                    power(xr[:], xs_[:], 2).then_inc(x_chain, 1)

            def u_rsqrt(b):
                pool.wait_ge(u_chain, after(U_STEPS, b, "te"))
                power(uv[:, 4, :], uv[:, 3, :], 2).then_inc(u_chain, 1)

            def h_rsqrt(b):
                pool.wait_ge(h_chain, after(H_STEPS, b, "ve"))
                power(h_rstd[:], h_ve[:], 2).then_inc(h_chain, 1)

            group_rsqrts(0, True)
            h_rsqrt(0)
            with pool.Fori(0, B - 1) as b:
                group_rsqrts(b + 1, True)
                u_rsqrt(b)
                h_rsqrt(b + 1)
            group_rsqrts(B, False)
            u_rsqrt(B - 1)

        @block.tensor
        def _(pe):
            def conv1_chunk(b, j, q):
                pe.wait_ge(x_loaded[q], 16 * (b * K + j + 1))
                for o in range(HALVES):
                    if not (isinstance(b, int) and isinstance(j, int) and b == 0 and j == 0 and q == 0):
                        pe.wait_ge(h_written, b * 2 * K + 4 * j + 2 * q + o - 1)
                    for n in range(2):
                        for i in range(HALVES):
                            mm = pe.matmul(ps_conv[:, o, n * BANK:(n + 1) * BANK],
                                           w1_s[:, i, o * P:(o + 1) * P],
                                           x_ring[:, q, i, n * BANK:(n + 1) * BANK],
                                           start=i == 0, stop=i == HALVES - 1)
                    mm.then_inc(conv1_done, 1)

            def conv1_phase(b):
                pe.wait_ge(x_chain, after(X_STEPS, b, "bias"))
                if not isinstance(b, int):
                    pe.wait_ge(a_chain, after(A_STEPS, b - 1, "sigmoid"))
                for q in range(2):
                    conv1_chunk(b, 0, q)
                with pe.Fori(1, K // 2) as j:
                    for q in range(2):
                        conv1_chunk(b, j, q)

            def conv2_weights(b):
                pe.wait_ge(h_chain, after(H_STEPS, b, "w1"))
                for o in range(HALVES):
                    for i in range(HALVES):
                        mm = pe.matmul(ps_b2[:, o:o + 1], w2_s[:, i, o * P:(o + 1) * P],
                                       h_mv[:, i, 0:1], start=i == 0, stop=i == HALVES - 1)
                mm.then_inc(h_chain, 1)

            def conv2_chunk(b, j, q, first=False):
                k = 2 * j + q
                if not first:
                    pe.wait_ge(x1_half, b * 2 * K + 2 * k)
                for o in range(HALVES):
                    for n in range(2):
                        for i in range(HALVES):
                            mm = pe.matmul(ps_conv[:, o, n * BANK:(n + 1) * BANK],
                                           w2_s[:, i, o * P:(o + 1) * P],
                                           rows(i, k * ROWS + 1 + n * BROWS, BROWS),
                                           start=i == 0, stop=i == HALVES - 1)
                mm.then_inc(conv2_done, 1)

            def dw_chunk(b, k, edge=None):
                pe.wait_ge(x1_half, b * 2 * K + 2 * (k + (1 if edge == "last" else 2)))
                for o in range(HALVES):
                    if edge != "first":
                        pe.wait_ge(u_written, b * 2 * K + 2 * k + o - 1)
                    for n in range(2):
                        for m, t in enumerate(PE_TAPS[o]):
                            dy, dx = TAPS[t]
                            mm = pe.matmul(ps_dw[:, o, n * BANK:(n + 1) * BANK], diag[:, o, m],
                                           rows(o, k * ROWS + 1 + dy + n * BROWS, BROWS, 1 + dx),
                                           start=m == 0, stop=m == len(PE_TAPS[o]) - 1)
                    mm.then_inc(dw_products, 1)

            def group_product(n, dst, src, before):
                pe.wait_ge(g_chain, after(G_STEPS, n, before))
                pe.matmul(dst, group[:], src, start=True, stop=True).then_inc(g_chain, 1)

            def x_bias(n):
                pe.wait_ge(x_chain, after(X_STEPS, n, "w1"))
                for o in range(HALVES):
                    for i in range(HALVES):
                        mm = pe.matmul(ps_b1[:, o:o + 1], w1_s[:, i, o * P:(o + 1) * P],
                                       mean[:, i:i + 1], start=i == 0, stop=i == HALVES - 1)
                mm.then_inc(x_chain, 1)

            def attention(b):
                pe.wait_ge(a_chain, after(A_STEPS, b, "pool"))
                for i in range(HALVES):
                    mm = pe.matmul(ps_hid, att1[:, i, :], pooled[:, i:i + 1],
                                   start=i == 0, stop=i == HALVES - 1)
                mm.then_inc(a_chain, 1)
                pe.wait_ge(a_chain, after(A_STEPS, b, "leaky"))
                for o in range(HALVES):
                    mm = pe.matmul(ps_at[:, o:o + 1], att2[:, o * P:(o + 1) * P], hidden[:],
                                   start=True, stop=True)
                mm.then_inc(a_chain, 1)

            def conv2_phase(b, last):
                conv2_weights(b)
                conv2_chunk(b, 0, 0, first=True)
                conv2_chunk(b, 0, 1)
                conv2_chunk(b, 1, 0)
                dw_chunk(b, 0, "first")
                conv2_chunk(b, 1, 1)
                dw_chunk(b, 1)
                with pe.Fori(2, K // 2) as j:
                    for q in range(2):
                        conv2_chunk(b, j, q)
                        dw_chunk(b, 2 * j + q - 2)
                dw_chunk(b, K - 2)
                group_product(b + 1, ps_gm, mean[:], "mean")
                group_product(b + 1, ps_gq, tmp4[:], "q")
                dw_chunk(b, K - 1, "last")
                if not last:
                    x_bias(b + 1)
                attention(b)

            pe.wait_ge(const_pool, 6)
            pe.wait_ge(const_loaded, 16 * 8)
            pe.wait_ge(const_dve, CONST_DVE)
            group_product(0, ps_gm, mean[:], "mean")
            group_product(0, ps_gq, tmp4[:], "q")
            x_bias(0)
            conv1_phase(0)
            with pe.Fori(0, B - 1) as b:
                conv2_phase(b, False)
                conv1_phase(b + 1)
            conv2_phase(B - 1, True)

        @block.scalar
        def _(act):
            def load_stat(b, k, q, wait=None):
                if wait is not None:
                    act.wait_ge(x_summed, wait)
                act.dma_start(stat_ring[:, q], xv[:, bass.ds(b * HALVES, HALVES), bass.ds(k * CP, CP)]
                              ).then_inc(stat_loaded[q], 16)

            def store_out(b, k, q, o):
                act.wait_ge(out_ready, b * 2 * K + 2 * k + o + 1)
                act.dma_start(ov[:, bass.ds(b * HALVES + o, 1), bass.ds(k * CP, CP)],
                              fin_ring[:, q, o:o + 1]).then_inc(out_stored[2 * q + o], 16)

            def x_sums(b, j, q, freed=None):
                act.wait_ge(stat_loaded[q], 16 * (b * (K // 2) + j + 1))
                k = 2 * j + q
                if freed is None:
                    nc.scalar.mul(neg_pivot[:, 0:2], stat_ring[:, 0, :, 0], -1.0).then_inc(x_pivot, 1)
                    act.wait_ge(x_pivot, b + 1)
                for o in range(HALVES):
                    src = stat_ring[:, q, o, :]
                    if freed is not None:
                        freed(o)
                    nc.scalar.activation(unused[:, 2 + o], src, ACT.Identity,
                                         accum_out=part[:, o, bass.ds(k, 1)])
                    nc.scalar.activation(src, src, ACT.Square,
                                         bias=neg_pivot[:, o:o + 1],
                                         accum_out=part[:, 4 + o, bass.ds(k, 1)]).then_inc(x_summed, 1)

            def after_x(b, k, o):
                act.wait_ge(x_summed, b * 2 * K + 2 * k + o + 1)

            def after_u(b, k, o):
                act.wait_ge(u_summed, b * 2 * K + 2 * k + o + 1)

            def after_x1(b, k, o):
                act.wait_ge(x1_squared, b * 2 * K + 2 * k + o + 1)

            def x1_squares(b, k, freed):
                for o in range(HALVES):
                    act.wait_ge(x1_half, b * 2 * K + 2 * k + o + 1)
                    if freed is not None:
                        freed(o)
                    nc.scalar.activation(grid(unused[:, o]), rows(o, k * ROWS + 1, ROWS), ACT.Square,
                                         bias=neg_pivot[:, 2 + o:3 + o],
                                         accum_out=part[:, 6 + o, bass.ds(k, 1)]).then_inc(x1_squared, 1)

            def u_sums(b, k, freed, skip_top=0, skip_bottom=0):
                n = ROWS - skip_top - skip_bottom
                for o in range(HALVES):
                    act.wait_ge(u_written, b * 2 * K + 2 * k + o + 1)
                    freed(o)
                    src = rows(o, k * ROWS + skip_top, n, 2, W - 2)
                    for m, func in enumerate((ACT.Identity, ACT.Square)):
                        dst = unused[:, 2 * (1 - o) + m]
                        made = nc.scalar.activation(grid(dst)[:, 0:n, 0:W - 2], src, func,
                                                    bias=u_neg_pivot[:, o:o + 1],
                                                    accum_out=u_part[:, 2 * m + o, bass.ds(k, 1)])
                    made.then_inc(u_summed, 1)

            def conv2_phase(b, last):
                def u_freed(k):
                    def freed(o):
                        if o == 1:
                            after_x1(b, k + 3, 1)
                        elif not last:
                            after_x(b + 1, k + 2, 1)
                        elif not isinstance(k, int):
                            after_u(b, k - 1, 0)
                    return freed

                def x_sums_next(j, q, freed):
                    if not last:
                        x_sums(b + 1, j, q, freed)

                if not last:
                    for q in range(2):
                        load_stat(b + 1, q, q, (b + 1) * 2 * K)
                x1_squares(b, 0, None)
                x_sums_next(0, 0, None)
                x_sums_next(0, 1, lambda o: after_x(b + 1, 0, o))
                x1_squares(b, 1, lambda o: after_x1(b, 0, o))
                if not last:
                    for q in range(2):
                        load_stat(b + 1, 2 + q, q, (b + 1) * 2 * K + 2 * (q + 1))
                x1_squares(b, 2, lambda o: after_x1(b, 1, o))
                x_sums_next(1, 0, lambda o: after_x(b + 1, 1, o))
                x1_squares(b, 3, lambda o: after_x1(b, 2, o))
                u_sums(b, 0, u_freed(0), skip_top=1)
                x_sums_next(1, 1, lambda o: after_u(b, 0, 0))
                with act.Fori(2, K // 2) as j:
                    for q in range(2):
                        k = 2 * j + q
                        if not last:
                            load_stat(b + 1, k, q, (b + 1) * 2 * K + 2 * (k - 1))
                        x1_squares(b, k, lambda o: after_u(b, k - 4, 1))
                        u_sums(b, k - 3, u_freed(k - 3))
                        x_sums_next(j, q, lambda o: after_u(b, k - 3, 0))
                u_sums(b, K - 3, lambda o: after_x(b + 1, K - 1, 1) if o == 0 and not last
                       else after_u(b, K - 4, o))
                act.wait_ge(a_chain, after(A_STEPS, b, "att"))
                nc.scalar.activation(attn[:], ps_at, ACT.Sigmoid).then_inc(a_chain, 1)
                u_sums(b, K - 2, lambda o: after_u(b, K - 3, o))
                u_sums(b, K - 1, lambda o: after_u(b, K - 2, o), skip_bottom=1)
                act.wait_ge(u_chain, after(U_STEPS, b, "corner"))
                for o in range(HALVES):
                    top_bottom = body[:, o, 0:H:H - 1, 1:W + 1]
                    left_right = body[:, o, 1:H - 1, 1:W + 1:W - 1]
                    for n, (src, r, w) in enumerate(((top_bottom, 2, W), (left_right, H - 2, 2))):
                        for m, func in enumerate((ACT.Identity, ACT.Square)):
                            dst = unused[:, 2 * n + m, o * 2 * W:o * 2 * W + r * w]
                            made = nc.scalar.activation(dst.rearrange("p (r w) -> p r w", w=w), src, func,
                                                        bias=u_neg_pivot[:, o:o + 1],
                                                        accum_out=u_part[:, 2 * m + o, K + n:K + n + 1])
                made.then_inc(edge_summed, 1)

            def relu_u(b, k, o):
                nc.scalar.activation(grid(ps_dw[:, o]), rows(o, k * ROWS, ROWS), ACT.Relu,
                                     bias=relu_shift[:, o:o + 1], scale=relu_scale[:, o:o + 1]
                                     ).then_inc(relu_done, 1)

            def write_h(b, k, o):
                act.wait_ge(conv1_done, b * 2 * K + 2 * k + o + 1)
                nc.scalar.activation(rows(o, k * ROWS + 1, ROWS), grid(ps_conv[:, o]), ACT.Relu,
                                     bias=bias1[:, o:o + 1]).then_inc(h_written, 1)

            def final_phase(b, conv1):
                def h_over_u(k):
                    for o in range(HALVES):
                        act.wait_ge(leaky_done, b * 2 * K + 2 * min_chunk(k) + o + 1)
                        write_h(b + 1, k, o)

                def min_chunk(k):
                    return k if isinstance(k, int) and k == K - 1 else k + 1

                def chunk(k, q):
                    for o in range(HALVES):
                        act.wait_ge(out_ready, b * 2 * K + 2 * k + o + 1)
                        relu_u(b, k + 1, o)
                    for o in range(HALVES):
                        store_out(b, k, q, o)
                    if conv1:
                        h_over_u(k)

                act.wait_ge(u_chain, after(U_STEPS, b, "last"))
                for o in range(HALVES):
                    relu_u(b, 0, o)
                with act.Fori(0, K // 2 - 1) as j:
                    for q in range(2):
                        chunk(2 * j + q, q)
                chunk(K - 2, 0)
                if conv1:
                    h_over_u(K - 1)
                for o in range(HALVES):
                    store_out(b, K - 1, 1, o)

            act.wait_ge(const_dve, CONST_CLEARED)
            for q in range(2):
                load_stat(0, q, q)
            x_sums(0, 0, 0)
            x_sums(0, 0, 1, lambda o: after_x(0, 0, o))
            with act.Fori(1, K // 2) as j:
                for q in range(2):
                    load_stat(0, 2 * j + q, q, 2 * (2 * j + q - 1))
                for q in range(2):
                    x_sums(0, j, q, lambda o: after_x(0, 2 * j + q - 1, o))
            with act.Fori(0, K) as k:
                for o in range(HALVES):
                    write_h(0, k, o)
            with act.Fori(0, B - 1) as b:
                conv2_phase(b, False)
                final_phase(b, True)
            conv2_phase(B - 1, True)
            final_phase(B - 1, False)
            for n in range(4):
                act.wait_ge(out_stored[n], 16 * B * (K // 2))

        @block.vector
        def _(dve):
            V = nc.vector

            def step(chain, steps, n, name, make):
                at = steps.index(name)
                if not (at == 0):
                    dve.wait_ge(chain, n * len(steps) + at)
                make().then_inc(chain, 1)

            def g_steps_to_mean(n):
                s = lambda name, make: step(g_chain, G_STEPS, n, name, make)
                s("total", lambda: V.reduce_sum(total[:], part[:], AX_X))
                s("dm", lambda: V.scalar_tensor_tensor(out=dm[:], in0=total[:, 0:4], scalar=1.0 / NPIX,
                                                       in1=neg_pivot[:], op0=ALU.mult, op1=ALU.add))
                s("dm2", lambda: V.tensor_tensor(tmp4[:], dm[:], dm[:], ALU.mult))
                s("var", lambda: V.scalar_tensor_tensor(out=var[:], in0=total[:, 4:8], scalar=1.0 / NPIX,
                                                        in1=tmp4[:], op0=ALU.mult, op1=ALU.subtract))
                s("var0", lambda: V.tensor_scalar(var[:], var[:], 0.0, None, ALU.max))
                s("mean", lambda: V.scalar_tensor_tensor(out=mean[:], in0=total[:, 0:4],
                                                         scalar=1.0 / NPIX, in1=add_back[:],
                                                         op0=ALU.mult, op1=ALU.add))

            def g_steps_to_q(n):
                s = lambda name, make: step(g_chain, G_STEPS, n, name, make)
                s("gmean", lambda: V.tensor_copy(gmean[:], ps_gm))
                s("dev", lambda: V.tensor_tensor(dev[:], mean[:], gmean[:], ALU.subtract))
                s("dev2", lambda: V.tensor_tensor(tmp4[:], dev[:], dev[:], ALU.mult))
                s("q", lambda: V.tensor_tensor(tmp4[:], tmp4[:], var[:], ALU.add))

            def g_steps_to_ve(n):
                step(g_chain, G_STEPS, n, "ve", lambda: V.tensor_scalar(tmp4[:], ps_gq, EPS, None, ALU.add))

            def x_steps_to_weights(n):
                s = lambda name, make: step(x_chain, X_STEPS, n, name, make)
                dve.wait_ge(g_chain, after(G_STEPS, n, "rstd"))
                s("t", lambda: V.tensor_tensor(xs_[:], var[:, 0:2], grstd[:, 0:2], ALU.mult))
                s("t2", lambda: V.tensor_tensor(xs_[:], xs_[:], grstd[:, 0:2], ALU.mult))
                s("te", lambda: V.tensor_scalar(xs_[:], xs_[:], EPS, None, ALU.add))
                dve.wait_ge(x_chain, after(X_STEPS, n, "rstd"))
                V.tensor_tensor(xs_[:], xr[:], grstd[:, 0:2], ALU.mult).then_inc(x_chain, 1)
                for i in range(HALVES):
                    s(f"w{i}", lambda i=i: V.tensor_scalar(w1_s[:, i, :], w1_raw[:, i, :],
                                                           xs_[:, i:i + 1], None, ALU.mult))

            def x_steps_to_end(n):
                s = lambda name, make: step(x_chain, X_STEPS, n, name, make)
                s("bias", lambda: V.tensor_tensor(bias1[:], b1c, ps_b1, ALU.subtract))
                s("pivots", lambda: V.tensor_scalar(neg_pivot[:, 2:4], mean[:, 0:2], -1.0, None, ALU.mult))
                s("upivot", lambda: V.tensor_tensor(u_neg_pivot[:], neg_pivot[:, 2:4], tap_sum[:], ALU.mult))

            def h_steps(b):
                s = lambda name, make: step(h_chain, H_STEPS, b, name, make)
                dve.wait_ge(h_counted, (b + 1) * 2 * K)
                s("top", lambda: V.memset(body[:, :, 0, :], 0.0))
                for i in range(HALVES):
                    V.bn_aggr(h_mv[:, i, :], h_stats[:, i].rearrange("p a b -> p (a b)")
                              ).then_inc(h_chain, 1)
                s("ve", lambda: V.tensor_scalar(h_ve[:], h_mv[:, :, 1], EPS, None, ALU.add))
                for i in range(HALVES):
                    s(f"w{i}", lambda i=i: V.tensor_scalar(w2_s[:, i, :], w2_raw[:, i, :],
                                                           h_rstd[:, i:i + 1], None, ALU.mult))
                s("neg", lambda: V.tensor_tensor(neg_beta2[:], ps_b2, b2c, ALU.subtract))
                s("beta", lambda: V.tensor_scalar(beta2[:], neg_beta2[:], -1.0, None, ALU.mult))
                dve.wait_ge(h_chain, after(H_STEPS, b, "beta"))
                V.tensor_copy(add_back[:, 2:4], beta2[:])

            def write_x1(b, j, q):
                k = 2 * j + q
                dve.wait_ge(conv2_done, b * K + k + 1)
                dve.wait_ge(x_loaded[q], 16 * (b * K + K // 2 + j + 1))
                for o in range(HALVES):
                    V.scalar_tensor_tensor(out=rows(o, k * ROWS + 1, ROWS), in0=grid(ps_conv[:, o]),
                                           scalar=neg_beta2[:, o:o + 1], in1=grid(x_ring[:, q, o]),
                                           op0=ALU.max, op1=ALU.add,
                                           accum_out=part[:, 2 + o, bass.ds(k, 1)]).then_inc(x1_half, 1)

            def write_u(b, k, j, q):
                taps_per_chunk = NT[0] + NT[1] - 2
                dve.wait_ge(dw_products, b * 2 * K + 2 * k + 2)
                dve.wait_ge(x1_squared, b * 2 * K + 2 * k + 2)
                dve.wait_ge(spilled[q], 32 * (b * (K // 2) + j + 1))
                done = 0
                for m in range(max(NT)):
                    for o in range(HALVES):
                        if m >= NT[o]:
                            continue
                        t = DVE_TAPS[o][m]
                        dy, dx = TAPS[t]
                        src = rows(o, k * ROWS + 1 + dy, ROWS, 1 + dx)
                        final = m == NT[o] - 1
                        if m > 0:
                            dve.wait_ge(tap_added, (b * K + k) * taps_per_chunk + done_at[o])
                        ins = V.scalar_tensor_tensor(
                            out=rows(o, k * ROWS, ROWS) if final else grid(ps_dw[:, o]),
                            in0=src, scalar=taps[:, o, t:t + 1], in1=grid(ps_dw[:, o]),
                            op0=ALU.mult, op1=ALU.add)
                        if final:
                            ins.then_inc(u_written, 1)
                        else:
                            ins.then_inc(tap_added, 1)
                            done += 1
                            done_at[o] = done

            done_at = [0, 0]

            def a_steps(b):
                s = lambda name, make: step(a_chain, A_STEPS, b, name, make)
                s("pool", lambda: V.tensor_tensor(pooled[:], dev[:, 2:4], grstd[:, 2:4], ALU.mult))
                s("copy", lambda: V.tensor_copy(hidden_raw[:], ps_hid))
                s("leaky", lambda: V.scalar_tensor_tensor(out=hidden[:], in0=hidden_raw[:], scalar=SLOPE,
                                                          in1=hidden_raw[:], op0=ALU.mult, op1=ALU.max))

            def a_steps_to_end(b):
                s = lambda name, make: step(a_chain, A_STEPS, b, name, make)
                s("alpha", lambda: V.tensor_tensor(alpha[:], attn[:], grstd[:, 2:4], ALU.mult))
                s("k", lambda: V.tensor_tensor(padk[:], gmean[:, 2:4], beta2[:], ALU.subtract))
                wide = padk[:].unsqueeze(2).to_broadcast([P, HALVES, 2])
                s("krows", lambda: V.tensor_tensor(k_rows[:], edge_rows[:], wide, ALU.mult))
                s("kcols", lambda: V.tensor_tensor(k_cols[:], edge_cols[:], wide, ALU.mult))
                corners = taps[:].rearrange("p o (y x) -> p o y x", x=3)[:, :, 0:3:2, 0:3:2]
                s("kcorner", lambda: V.tensor_tensor(
                    k_corner[:], corners,
                    padk[:].unsqueeze(2).unsqueeze(3).to_broadcast([P, HALVES, 2, 2]), ALU.mult))

            def u_steps(b):
                s = lambda name, make: step(u_chain, U_STEPS, b, name, make)
                dve.wait_ge(a_chain, after(A_STEPS, b, "kcorner"))
                dve.wait_ge(u_summed, (b + 1) * 2 * K)
                tb = body[:, :, 0:H:H - 1, 1:W + 1]
                s("rows", lambda: V.tensor_tensor(tb, tb, k_rows[:].unsqueeze(3).to_broadcast([P, 2, 2, W]), ALU.add))
                lr = body[:, :, 0:H, 1:W + 1:W - 1]
                s("cols", lambda: V.tensor_tensor(lr, lr, k_cols[:].unsqueeze(2).to_broadcast([P, 2, H, 2]), ALU.add))
                cc = body[:, :, 0:H:H - 1, 1:W + 1:W - 1]
                s("corner", lambda: V.tensor_tensor(cc, cc, k_corner[:], ALU.subtract))
                dve.wait_ge(edge_summed, b + 1)
                v = lambda i: uv[:, i, :]
                s("total", lambda: V.reduce_sum(u_total[:], u_part[:], AX_X))
                s("m", lambda: V.tensor_scalar(v(0), u_total[:, 0:2], 1.0 / NPIX, None, ALU.mult))
                s("m2", lambda: V.tensor_tensor(v(1), v(0), v(0), ALU.mult))
                s("var", lambda: V.scalar_tensor_tensor(out=v(1), in0=u_total[:, 2:4], scalar=1.0 / NPIX,
                                                        in1=v(1), op0=ALU.mult, op1=ALU.subtract))
                s("var0", lambda: V.tensor_scalar(v(1), v(1), 0.0, None, ALU.max))
                s("mean", lambda: V.tensor_tensor(v(0), v(0), u_neg_pivot[:], ALU.subtract))
                s("t", lambda: V.tensor_tensor(v(3), v(1), alpha[:], ALU.mult))
                s("t2", lambda: V.tensor_tensor(v(3), v(3), alpha[:], ALU.mult))
                s("te", lambda: V.tensor_scalar(v(3), v(3), EPS, None, ALU.add))
                s("scale", lambda: V.tensor_tensor(u_scale[:], alpha[:], v(4), ALU.mult))
                s("kw", lambda: V.tensor_tensor(v(5), padk[:], tap_sum[:], ALU.mult))
                s("akw", lambda: V.tensor_tensor(v(5), v(5), alpha[:], ALU.mult))
                s("c0", lambda: V.tensor_tensor(v(5), rbc, v(5), ALU.subtract))
                s("am", lambda: V.tensor_tensor(v(6), alpha[:], v(0), ALU.mult))
                s("mu", lambda: V.tensor_tensor(v(6), v(6), v(5), ALU.add))
                s("d", lambda: V.tensor_tensor(v(7), v(5), v(6), ALU.subtract))
                s("shift", lambda: V.tensor_tensor(u_shift[:], v(7), v(4), ALU.mult))
                s("scale99", lambda: V.tensor_scalar(relu_scale[:], u_scale[:], 1.0 - SLOPE, None, ALU.mult))
                s("shift99", lambda: V.tensor_scalar(relu_shift[:], u_shift[:], 1.0 - SLOPE, None, ALU.mult))
                s("scale01", lambda: V.tensor_scalar(slope_scale[:], u_scale[:], SLOPE, None, ALU.mult))
                s("last", lambda: V.scalar_tensor_tensor(out=out_shift[:], in0=u_shift[:], scalar=SLOPE,
                                                         in1=beta2[:], op0=ALU.mult, op1=ALU.add))

            def conv2_phase(b, last):
                write_x1(b, 0, 0)
                write_x1(b, 0, 1)
                write_x1(b, 1, 0)
                write_u(b, 0, 0, 0)
                write_x1(b, 1, 1)
                write_u(b, 1, 0, 1)
                with dve.Fori(2, K // 2) as j:
                    for q in range(2):
                        write_x1(b, j, q)
                        write_u(b, 2 * j + q - 2, j - 1, q)
                dve.wait_ge(x1_squared, (b + 1) * 2 * K)
                dve.wait_ge(x_summed, (b + 2) * 2 * K if not last else B * 2 * K)
                g_steps_to_mean(b + 1)
                write_u(b, K - 2, K // 2 - 1, 0)
                g_steps_to_q(b + 1)
                g_steps_to_ve(b + 1)
                write_u(b, K - 1, K // 2 - 1, 1)
                dve.wait_ge(g_chain, after(G_STEPS, b + 1, "rstd"))
                if not last:
                    x_steps_to_weights(b + 1)
                a_steps(b)
                a_steps_to_end(b)
                u_steps(b)
                if not last:
                    x_steps_to_end(b + 1)

            def make_out(b, j, q):
                at = b * 2 * K + 4 * j + 2 * q
                for o in range(HALVES):
                    dve.wait_ge(relu_done, at + o + 1)
                    V.scalar_tensor_tensor(out=grid(ps_dw[:, o]), in0=rows(o, (2 * j + q) * ROWS, ROWS),
                                           scalar=slope_scale[:, o:o + 1], in1=grid(ps_dw[:, o]),
                                           op0=ALU.mult, op1=ALU.add).then_inc(leaky_done, 1)
                for o in range(HALVES):
                    dve.wait_ge(fin_loaded[2 * q + o], 16 * (b * (K // 2) + j + 1))
                    dve.wait_ge(leaky_done, at + o + 1)
                    V.scalar_tensor_tensor(out=fin_ring[:, q, o], in0=ps_dw[:, o],
                                           scalar=out_shift[:, o:o + 1], in1=fin_ring[:, q, o],
                                           op0=ALU.add, op1=ALU.add).then_inc(out_ready, 1)

            def count_h(b, j, q):
                for o in range(HALVES):
                    dve.wait_ge(h_written, b * 2 * K + 4 * j + 2 * q + o + 1)
                    for n in range(2):
                        k2 = 4 * j + 2 * q + n
                        ins = V.bn_stats(h_stats[:, o, bass.ds(k2, 1), :].rearrange("p a b -> p (a b)"),
                                         rows(o, 2 * (2 * j + q) * BROWS + 1 + n * BROWS, BROWS))
                    ins.then_inc(h_counted, 1)

            V.memset(part[:], 0.0).then_inc(const_dve, 1)
            V.memset(neg_pivot[:, 2:4], 0.0).then_inc(const_dve, 1)
            V.memset(add_back[:], 0.0).then_inc(const_dve, 1)
            V.memset(body[:], 0.0).then_inc(const_dve, 1)
            dve.wait_ge(const_loaded, 16 * 8)
            dve.wait_ge(const_pool, 6)
            for o in range(HALVES):
                for m, t in enumerate(PE_TAPS[o]):
                    V.tensor_scalar(diag[:, o, m, :], ident[:], taps[:, o, t:t + 1], None, ALU.mult
                                    ).then_inc(const_dve, 1)
            V.reduce_sum(edge_rows[:], taps[:].rearrange("p o (y x) -> p o y x", x=3)[:, :, 0:3:2, :],
                         AX_X).then_inc(const_dve, 1)
            V.reduce_sum(edge_cols[:], taps[:].rearrange("p o (y x) -> p o x y", x=3)[:, :, 0:3:2, :],
                         AX_X).then_inc(const_dve, 1)
            V.reduce_sum(tap_sum[:], taps[:], AX_X).then_inc(const_dve, 1)

            dve.wait_ge(const_dve, CONST_DVE)
            dve.wait_ge(x_summed, 2 * K)
            g_steps_to_mean(0)
            g_steps_to_q(0)
            g_steps_to_ve(0)
            x_steps_to_weights(0)
            x_steps_to_end(0)
            with dve.Fori(0, K // 2) as j:
                for q in range(2):
                    count_h(0, j, q)
            h_steps(0)
            with dve.Fori(0, B - 1) as b:
                conv2_phase(b, False)
                make_out(b, 0, 0)
                make_out(b, 0, 1)
                count_h(b + 1, 0, 0)
                with dve.Fori(1, K // 2) as j:
                    for q in range(2):
                        make_out(b, j, q)
                        count_h(b + 1, j - 1 + q, 1 - q)
                count_h(b + 1, K // 2 - 1, 1)
                h_steps(b + 1)
            conv2_phase(B - 1, True)
            with dve.Fori(0, K // 2) as j:
                for q in range(2):
                    make_out(B - 1, j, q)


def kernel(**inputs):
    import numpy as np
    import concourse.bacc as bacc
    from concourse.bass_utils import run_bass_kernel_spmd

    C = inputs["x"].shape[1]
    column = lambda a: np.ascontiguousarray(np.asarray(a).reshape(2, C // 2).T)
    arrays = {
        "x": np.ascontiguousarray(inputs["x"]),
        "w1t": np.ascontiguousarray(np.asarray(inputs["L0_conv_w1"]).T),
        "b1": column(inputs["L0_conv_b1"]),
        "w2t": np.ascontiguousarray(np.asarray(inputs["L0_conv_w2"]).T),
        "b2": column(inputs["L0_conv_b2"]),
        "a1t": np.ascontiguousarray(np.asarray(inputs["L1_conv_attn_w1"]).T),
        "a2t": np.ascontiguousarray(np.asarray(inputs["L1_conv_attn_w2"]).T),
        "rw": np.ascontiguousarray(np.asarray(inputs["L1_conv_refine_w"]).reshape(C, 9)),
        "rb": column(inputs["L1_conv_refine_b"]),
    }
    nc = bacc.Bacc("TRN2", target_bir_lowering=False, num_devices=1)
    aps = [nc.dram_tensor(f"in_{n}", a.shape, mybir.dt.from_np(a.dtype), kind="ExternalInput").ap()
           for n, a in arrays.items()]
    out = nc.dram_tensor("out_0", inputs["x"].shape, F32, kind="ExternalOutput").ap()
    conv_preact_kernel(nc, *aps, out)
    r = run_bass_kernel_spmd(nc, [{f"in_{n}": a for n, a in arrays.items()}], core_ids=[0])
    return r.results[0]["out_0"]
```

```python
from contextlib import ExitStack

import concourse.bass as bass
from concourse import mybir

ALU = mybir.AluOpType
ACT = mybir.ActivationFunctionType
F32 = mybir.dt.float32
AX_X = mybir.AxisListType.X

P = 128
EPS = 1e-5
SLOPE = 0.01
TAPS = [(dy, dx) for dy in (-1, 0, 1) for dx in (-1, 0, 1)]
PE_TAPS = [[4, 1, 7], [4, 1, 7]]
DVE_TAPS = [[t for t in range(9) if t not in PE_TAPS[o]] for o in range(2)]


def conv_preact_kernel(nc, x, w1t, b1, w2t, b2, a1t, a2t, rw, rb, out):
    B, C, H, W = x.shape
    HALVES = C // P
    HID = a1t.shape[1]
    GROUP = C // 32
    ROWS = 8
    CP = ROWS * W
    K = H // ROWS
    BANK = 512
    BROWS = BANK // W
    NPIX = H * W
    PITCH = W + 2
    NT = [len(DVE_TAPS[o]) for o in range(HALVES)]
    assert HALVES == 2 and CP == 2 * BANK and K % 2 == 0

    xv = x.rearrange("b (o p) h w -> p (b o) (h w)", p=P)
    ov = out.rearrange("b (o p) h w -> p (b o) (h w)", p=P)
    x1_dram = nc.dram_tensor("x1_dram", [B, C, NPIX], F32, kind="Internal").ap()
    x1v = x1_dram.rearrange("b (o p) n -> p (b o) n", p=P)

    with ExitStack() as ctx:
        def sb(name, shape):
            return ctx.enter_context(nc.sbuf_tensor(name, shape, F32))

        def sem(name):
            return ctx.enter_context(nc.semaphore(name))

        body = sb("body", [P, HALVES, H + 2, PITCH])
        x_ring = sb("x_ring", [P, 2, HALVES, CP])
        stat_ring = sb("stat_ring", [P, 2, HALVES, CP])
        fin_ring = sb("fin_ring", [P, 2, HALVES, CP])
        unused = ctx.enter_context(nc.sbuf_tensor("unused", [P, 4, CP], mybir.dt.bfloat16))
        w1_raw = sb("w1_raw", [P, HALVES, C])
        w2_raw = sb("w2_raw", [P, HALVES, C])
        w1_s = sb("w1_s", [P, HALVES, C])
        w2_s = sb("w2_s", [P, HALVES, C])
        att1 = sb("att1", [P, HALVES, HID])
        att2 = sb("att2", [HID, C])
        taps = sb("taps", [P, HALVES, 9])
        vecs = sb("vecs", [P, 3, HALVES])
        b1c, b2c, rbc = (vecs[:, i, :] for i in range(3))
        ident = sb("ident", [P, P])
        group = sb("group", [P, P])
        diag = sb("diag", [P, HALVES, max(map(len, PE_TAPS)), P])
        minus_half = sb("minus_half", [P, 4])
        tap_sum = sb("tap_sum", [P, HALVES])
        edge_rows = sb("edge_rows", [P, HALVES, 2])
        edge_cols = sb("edge_cols", [P, HALVES, 2])
        part = sb("part", [P, 8, K])
        total = sb("total", [P, 8])
        u_part = sb("u_part", [P, 4, K + 2])
        u_total = sb("u_total", [P, 4])
        h_stats = sb("h_stats", [P, HALVES, 2 * K, 6])
        h_mv = sb("h_mv", [P, HALVES, 2])
        h_ve = sb("h_ve", [P, HALVES])
        h_rstd = sb("h_rstd", [P, HALVES])
        beta2 = sb("beta2", [P, HALVES])
        neg_beta2 = sb("neg_beta2", [P, HALVES])
        bias1 = sb("bias1", [P, HALVES])
        neg_pivot = sb("neg_pivot", [P, 4])
        add_back = sb("add_back", [P, 4])
        dm = sb("dm", [P, 4])
        var = sb("var", [P, 4])
        mean = sb("mean", [P, 4])
        gmean = sb("gmean", [P, 4])
        dev = sb("dev", [P, 4])
        tmp4 = sb("tmp4", [P, 4])
        grstd = sb("grstd", [P, 4])
        xs_ = sb("xs_", [P, HALVES])
        xr = sb("xr", [P, HALVES])
        pooled = sb("pooled", [P, HALVES])
        hidden_raw = sb("hidden_raw", [HID, 1])
        hidden = sb("hidden", [HID, 1])
        attn = sb("attn", [P, HALVES])
        alpha = sb("alpha", [P, HALVES])
        padk = sb("padk", [P, HALVES])
        u_neg_pivot = sb("u_neg_pivot", [P, HALVES])
        k_rows = sb("k_rows", [P, HALVES, 2])
        k_cols = sb("k_cols", [P, HALVES, 2])
        k_corner = sb("k_corner", [P, HALVES, 2, 2])
        uv = sb("uv", [P, 8, HALVES])
        relu_scale = sb("relu_scale", [P, HALVES])
        relu_shift = sb("relu_shift", [P, HALVES])
        slope_scale = sb("slope_scale", [P, HALVES])
        out_shift = sb("out_shift", [P, HALVES])

        ps_conv = ctx.enter_context(nc.psum_tensor("ps_conv", [P, HALVES, CP], F32))
        ps_dw = ctx.enter_context(nc.psum_tensor("ps_dw", [P, HALVES, CP], F32))
        ps_gm, ps_gq = ps_conv[:, 0, 0:4], ps_conv[:, 0, 4:8]
        ps_b1 = ps_conv[:, 0, BANK:BANK + 2]
        ps_hid = ps_conv[0:HID, 1, 0:1]
        ps_at = ps_conv[:, 1, BANK:BANK + 2]
        ps_b2 = ps_dw[:, 1, 0:2]

        const_loaded = sem("const_loaded")
        const_pool = sem("const_pool")
        const_dve = sem("const_dve")
        x_loaded = [sem(f"x_loaded{q}") for q in range(2)]
        stat_loaded = [sem(f"stat_loaded{q}") for q in range(2)]
        fin_loaded = [sem(f"fin_loaded{n}") for n in range(4)]
        out_stored = [sem(f"out_stored{n}") for n in range(4)]
        spilled = [sem(f"spilled{q}") for q in range(2)]
        conv1_done = sem("conv1_done")
        h_written = sem("h_written")
        conv2_done = sem("conv2_done")
        x1_half = sem("x1_half")
        x1_squared = sem("x1_squared")
        dw_products = sem("dw_products")
        tap_added = sem("tap_added")
        u_written = sem("u_written")
        u_summed = sem("u_summed")
        x_pivot = sem("x_pivot")
        x_summed = sem("x_summed")
        relu_done = sem("relu_done")
        leaky_done = sem("leaky_done")
        out_ready = sem("out_ready")
        h_counted = sem("h_counted")
        h_chain = sem("h_chain")
        g_chain = sem("g_chain")
        x_chain = sem("x_chain")
        a_chain = sem("a_chain")
        u_chain = sem("u_chain")
        edge_summed = sem("edge_summed")
        m_chain = sem("m_chain")

        H_STEPS = ["top", "aggr0", "aggr1", "ve", "rstd", "w0", "w1", "prod", "neg", "beta"]
        G_STEPS = ["total", "dm", "dm2", "var", "var0", "mean", "prod", "gmean", "dev", "dev2",
                   "q", "prod2", "ve", "rstd"]
        X_STEPS = ["t", "t2", "te", "rstd", "s", "w0", "w1", "prod", "bias", "pivots", "upivot"]
        A_STEPS = ["pool", "hid", "copy", "leaky", "att", "sigmoid", "alpha", "k", "krows", "kcols",
                   "kcorner", "kw", "akw", "c0"]
        U_STEPS = ["top", "cols", "corner", "bottom0", "cols0", "corner0", "bottom1", "cols1",
                   "corner1", "total", "m", "m2", "var", "vt", "vt2", "te", "rstd", "rscale", "rshift",
                   "sscale", "oshift", "last"]
        M_STEPS = ["mean", "am", "mu", "d"]

        CONST_CLEARED = 4
        CONST_DVE = CONST_CLEARED + sum(map(len, PE_TAPS)) + 3

        def after(steps, n, name):
            return n * len(steps) + steps.index(name) + 1

        def rows(o, first, count, c0=1, cn=W):
            return body[:, o, bass.ds(first, count), c0:c0 + cn]

        def grid(ap):
            return ap.rearrange("p (r w) -> p r w", w=W)

        block = ctx.enter_context(nc.Block())

        @block.sync
        def _(sp):
            for dst, src in ((w1_raw[:], w1t.rearrange("(o p) n -> p o n", p=P)),
                             (w2_raw[:], w2t.rearrange("(o p) n -> p o n", p=P)),
                             (att1[:], a1t.rearrange("(o p) n -> p o n", p=P)),
                             (att2[:], a2t),
                             (taps[:], rw.rearrange("(o p) t -> p o t", p=P)),
                             (b1c, b1), (b2c, b2), (rbc, rb)):
                sp.dma_start(dst, src).then_inc(const_loaded, 16)

            def load_x(b, k, q):
                sp.dma_start(x_ring[:, q], xv[:, bass.ds(b * HALVES, HALVES), bass.ds(k * CP, CP)]
                             ).then_inc(x_loaded[q], 16)

            def load_fin(b, k, q):
                for o in range(HALVES):
                    sp.dma_start(fin_ring[:, q, o:o + 1],
                                 x1v[:, bass.ds(b * HALVES + o, 1), bass.ds(k * CP, CP)]
                                 ).then_inc(fin_loaded[2 * q + o], 16)

            def reload_fin(b, k, j, q):
                for o in range(HALVES):
                    sp.wait_ge(out_stored[2 * q + o], 16 * (b * (K // 2) + j))
                load_fin(b, k, q)

            def conv1_streams(b, final):
                with sp.Fori(1, K // 2) as j:
                    for q in range(2):
                        k = 2 * j + q
                        sp.wait_ge(conv1_done, b * 2 * K + 2 * (k - 1))
                        load_x(b, k, q)
                        if final:
                            reload_fin(b - 1, k, j, q)
                for q in range(2):
                    sp.wait_ge(conv1_done, b * 2 * K + 2 * (K - 1 + q))
                    load_x(b, q, q)

            def spill_x1(b, k, q):
                sp.wait_ge(x1_half, b * 2 * K + 2 * (k + 1))
                for o in range(HALVES):
                    sp.dma_start(x1v[:, bass.ds(b * HALVES + o, 1), bass.ds(k * CP, CP)]
                                 .rearrange("p a (r w) -> p (a r) w", w=W),
                                 rows(o, k * ROWS + 1, ROWS)).then_inc(spilled[q], 16)

            def conv2_streams(b, last):
                with sp.Fori(0, K // 2 - 1) as j:
                    for q in range(2):
                        k = 2 * j + q
                        spill_x1(b, k, q)
                        load_x(b, k + 2, q)
                for q in range(2):
                    spill_x1(b, K - 2 + q, q)
                    if not last:
                        load_x(b + 1, q, q)
                for q in range(2):
                    sp.wait_ge(spilled[q], 32 * (b + 1) * (K // 2))
                    for o in range(HALVES):
                        if not (isinstance(b, int) and b == 0):
                            sp.wait_ge(out_stored[2 * q + o], 16 * b * (K // 2))
                    load_fin(b, q, q)

            for q in range(2):
                load_x(0, q, q)
            conv1_streams(0, False)
            conv2_streams(0, False)
            with sp.Fori(1, B - 1) as b:
                conv1_streams(b, True)
                conv2_streams(b, False)
            conv1_streams(B - 1, True)
            conv2_streams(B - 1, True)
            with sp.Fori(1, K // 2) as j:
                for q in range(2):
                    reload_fin(B - 1, 2 * j + q, j, q)

        @block.gpsimd
        def _(pool):
            nc.gpsimd.memset(ident[:], 0.0).then_inc(const_pool, 1)
            nc.gpsimd.memset(group[:], 1.0 / GROUP).then_inc(const_pool, 1)
            nc.gpsimd.memset(minus_half[:], -0.5).then_inc(const_pool, 1)
            pool.wait_ge(const_pool, 3)
            nc.gpsimd.affine_select(out=ident[:], in_=ident[:], compare_op=ALU.not_equal, fill=1.0,
                                    base=0, pattern=[[-1, P]], channel_multiplier=1
                                    ).then_inc(const_pool, 1)
            blocks = group[:].rearrange("p (g c) -> p g c", c=GROUP)
            nc.gpsimd.affine_select(out=blocks, in_=blocks, compare_op=ALU.is_ge, fill=0.0, base=0,
                                    pattern=[[-GROUP, P // GROUP], [0, GROUP]], channel_multiplier=1
                                    ).then_inc(const_pool, 1)
            pool.wait_ge(const_pool, 5)
            nc.gpsimd.affine_select(out=blocks, in_=blocks, compare_op=ALU.is_ge, fill=0.0,
                                    base=GROUP - 1, pattern=[[GROUP, P // GROUP], [0, GROUP]],
                                    channel_multiplier=-1).then_inc(const_pool, 1)

            def power(out_, in_, n):
                return nc.gpsimd.tensor_tensor(out_, in_, minus_half[:, 0:n], ALU.pow)

            def group_rsqrts(n, with_x):
                pool.wait_ge(g_chain, after(G_STEPS, n, "ve"))
                power(grstd[:], tmp4[:], 4).then_inc(g_chain, 1)
                if with_x:
                    pool.wait_ge(x_chain, after(X_STEPS, n, "te"))
                    power(xr[:], xs_[:], 2).then_inc(x_chain, 1)

            def u_rsqrt(b):
                pool.wait_ge(u_chain, after(U_STEPS, b, "te"))
                power(uv[:, 4, :], uv[:, 3, :], 2).then_inc(u_chain, 1)

            def h_rsqrt(b):
                pool.wait_ge(h_chain, after(H_STEPS, b, "ve"))
                power(h_rstd[:], h_ve[:], 2).then_inc(h_chain, 1)

            group_rsqrts(0, True)
            h_rsqrt(0)
            with pool.Fori(0, B - 1) as b:
                group_rsqrts(b + 1, True)
                u_rsqrt(b)
                h_rsqrt(b + 1)
            group_rsqrts(B, False)
            u_rsqrt(B - 1)

        @block.tensor
        def _(pe):
            def conv1_chunk(b, j, q):
                pe.wait_ge(x_loaded[q], 16 * (b * K + j + 1))
                for o in range(HALVES):
                    if not (isinstance(b, int) and isinstance(j, int) and b == 0 and j == 0 and q == 0):
                        pe.wait_ge(h_written, b * 2 * K + 4 * j + 2 * q + o - 1)
                    for n in range(2):
                        for i in range(HALVES):
                            mm = pe.matmul(ps_conv[:, o, n * BANK:(n + 1) * BANK],
                                           w1_s[:, i, o * P:(o + 1) * P],
                                           x_ring[:, q, i, n * BANK:(n + 1) * BANK],
                                           start=i == 0, stop=i == HALVES - 1)
                    mm.then_inc(conv1_done, 1)

            def conv1_phase(b):
                pe.wait_ge(x_chain, after(X_STEPS, b, "bias"))
                if not isinstance(b, int):
                    pe.wait_ge(a_chain, after(A_STEPS, b - 1, "sigmoid"))
                for q in range(2):
                    conv1_chunk(b, 0, q)
                with pe.Fori(1, K // 2) as j:
                    for q in range(2):
                        conv1_chunk(b, j, q)

            def conv2_weights(b):
                pe.wait_ge(h_chain, after(H_STEPS, b, "w1"))
                for o in range(HALVES):
                    for i in range(HALVES):
                        mm = pe.matmul(ps_b2[:, o:o + 1], w2_s[:, i, o * P:(o + 1) * P],
                                       h_mv[:, i, 0:1], start=i == 0, stop=i == HALVES - 1)
                mm.then_inc(h_chain, 1)

            def conv2_chunk(b, j, q, first=False):
                k = 2 * j + q
                if not first:
                    pe.wait_ge(x1_half, b * 2 * K + 2 * k)
                for o in range(HALVES):
                    for n in range(2):
                        for i in range(HALVES):
                            mm = pe.matmul(ps_conv[:, o, n * BANK:(n + 1) * BANK],
                                           w2_s[:, i, o * P:(o + 1) * P],
                                           rows(i, k * ROWS + 1 + n * BROWS, BROWS),
                                           start=i == 0, stop=i == HALVES - 1)
                mm.then_inc(conv2_done, 1)

            def dw_half(b, k, o, edge=None):
                pe.wait_ge(x1_half, b * 2 * K + 2 * (k + (1 if edge == "last" else 2)))
                if edge != "first":
                    pe.wait_ge(u_written, b * 2 * K + 2 * k + o - 1)
                for n in range(2):
                    for m, t in enumerate(PE_TAPS[o]):
                        dy, dx = TAPS[t]
                        mm = pe.matmul(ps_dw[:, o, n * BANK:(n + 1) * BANK], diag[:, o, m],
                                       rows(o, k * ROWS + 1 + dy + n * BROWS, BROWS, 1 + dx),
                                       start=m == 0, stop=m == len(PE_TAPS[o]) - 1)
                mm.then_inc(dw_products, 1)

            def dw_chunk(b, k, edge=None):
                for o in range(HALVES):
                    dw_half(b, k, o, edge)

            def group_product(n, dst, src, before):
                pe.wait_ge(g_chain, after(G_STEPS, n, before))
                pe.matmul(dst, group[:], src, start=True, stop=True).then_inc(g_chain, 1)

            def x_bias(n):
                pe.wait_ge(x_chain, after(X_STEPS, n, "w1"))
                for o in range(HALVES):
                    for i in range(HALVES):
                        mm = pe.matmul(ps_b1[:, o:o + 1], w1_s[:, i, o * P:(o + 1) * P],
                                       mean[:, i:i + 1], start=i == 0, stop=i == HALVES - 1)
                mm.then_inc(x_chain, 1)

            def attention_hidden(b):
                pe.wait_ge(a_chain, after(A_STEPS, b, "pool"))
                for i in range(HALVES):
                    mm = pe.matmul(ps_hid, att1[:, i, :], pooled[:, i:i + 1],
                                   start=i == 0, stop=i == HALVES - 1)
                mm.then_inc(a_chain, 1)

            def attention_out(b):
                pe.wait_ge(a_chain, after(A_STEPS, b, "leaky"))
                for o in range(HALVES):
                    mm = pe.matmul(ps_at[:, o:o + 1], att2[:, o * P:(o + 1) * P], hidden[:],
                                   start=True, stop=True)
                mm.then_inc(a_chain, 1)

            def conv2_phase(b, last):
                conv2_weights(b)
                conv2_chunk(b, 0, 0, first=True)
                conv2_chunk(b, 0, 1)
                conv2_chunk(b, 1, 0)
                dw_chunk(b, 0, "first")
                conv2_chunk(b, 1, 1)
                dw_chunk(b, 1)
                with pe.Fori(2, K // 2) as j:
                    for q in range(2):
                        conv2_chunk(b, j, q)
                        dw_chunk(b, 2 * j + q - 2)
                dw_half(b, K - 2, 0)
                group_product(b + 1, ps_gm, mean[:], "mean")
                group_product(b + 1, ps_gq, tmp4[:], "q")
                dw_half(b, K - 2, 1)
                if not last:
                    x_bias(b + 1)
                attention_hidden(b)
                dw_half(b, K - 1, 0, "last")
                attention_out(b)
                dw_half(b, K - 1, 1, "last")

            pe.wait_ge(const_pool, 6)
            pe.wait_ge(const_loaded, 16 * 8)
            pe.wait_ge(const_dve, CONST_DVE)
            group_product(0, ps_gm, mean[:], "mean")
            group_product(0, ps_gq, tmp4[:], "q")
            x_bias(0)
            conv1_phase(0)
            with pe.Fori(0, B - 1) as b:
                conv2_phase(b, False)
                conv1_phase(b + 1)
            conv2_phase(B - 1, True)

        @block.scalar
        def _(act):
            def load_stat(b, k, q, wait=None):
                if wait is not None:
                    act.wait_ge(x_summed, wait)
                act.dma_start(stat_ring[:, q], xv[:, bass.ds(b * HALVES, HALVES), bass.ds(k * CP, CP)]
                              ).then_inc(stat_loaded[q], 16)

            def store_out(b, k, q, o):
                act.wait_ge(out_ready, b * 2 * K + 2 * k + o + 1)
                act.dma_start(ov[:, bass.ds(b * HALVES + o, 1), bass.ds(k * CP, CP)],
                              fin_ring[:, q, o:o + 1]).then_inc(out_stored[2 * q + o], 16)

            def x_sums(b, j, q, freed=None):
                act.wait_ge(stat_loaded[q], 16 * (b * (K // 2) + j + 1))
                k = 2 * j + q
                if freed is None:
                    nc.scalar.mul(neg_pivot[:, 0:2], stat_ring[:, 0, :, 0], -1.0).then_inc(x_pivot, 1)
                    act.wait_ge(x_pivot, b + 1)
                for o in range(HALVES):
                    src = stat_ring[:, q, o, :]
                    if freed is not None:
                        freed(o)
                    nc.scalar.activation(unused[:, 2 + o], src, ACT.Identity,
                                         accum_out=part[:, o, bass.ds(k, 1)])
                    nc.scalar.activation(src, src, ACT.Square,
                                         bias=neg_pivot[:, o:o + 1],
                                         accum_out=part[:, 4 + o, bass.ds(k, 1)]).then_inc(x_summed, 1)

            def after_x(b, k, o):
                act.wait_ge(x_summed, b * 2 * K + 2 * k + o + 1)

            def after_u(b, k, o):
                act.wait_ge(u_summed, b * 2 * K + 2 * k + o + 1)

            def after_x1(b, k, o):
                act.wait_ge(x1_squared, b * 2 * K + 2 * k + o + 1)

            def x1_squares(b, k, freed):
                for o in range(HALVES):
                    act.wait_ge(x1_half, b * 2 * K + 2 * k + o + 1)
                    if freed is not None:
                        freed(o)
                    nc.scalar.activation(grid(unused[:, o]), rows(o, k * ROWS + 1, ROWS), ACT.Square,
                                         bias=neg_pivot[:, 2 + o:3 + o],
                                         accum_out=part[:, 6 + o, bass.ds(k, 1)]).then_inc(x1_squared, 1)

            def u_sums(b, k, freed, skip_top=0):
                n = ROWS - skip_top
                for o in range(HALVES):
                    act.wait_ge(u_written, b * 2 * K + 2 * k + o + 1)
                    freed(o)
                    src = rows(o, k * ROWS + skip_top, n, 2, W - 2)
                    for m, func in enumerate((ACT.Identity, ACT.Square)):
                        dst = unused[:, 2 * (1 - o) + m]
                        made = nc.scalar.activation(grid(dst)[:, 0:n, 0:W - 2], src, func,
                                                    bias=u_neg_pivot[:, o:o + 1],
                                                    accum_out=u_part[:, 2 * m + o, bass.ds(k, 1)])
                    made.then_inc(u_summed, 1)

            def conv2_phase(b, last):
                def u_freed(k):
                    def freed(o):
                        if o == 1:
                            after_x1(b, k + 3, 1)
                        elif not last:
                            after_x(b + 1, k + 2, 1)
                        elif not isinstance(k, int):
                            after_u(b, k - 1, 0)
                    return freed

                def x_sums_next(j, q, freed):
                    if not last:
                        x_sums(b + 1, j, q, freed)

                if not last:
                    for q in range(2):
                        load_stat(b + 1, q, q, (b + 1) * 2 * K)
                x1_squares(b, 0, None)
                x_sums_next(0, 0, None)
                x_sums_next(0, 1, lambda o: after_x(b + 1, 0, o))
                x1_squares(b, 1, lambda o: after_x1(b, 0, o))
                if not last:
                    for q in range(2):
                        load_stat(b + 1, 2 + q, q, (b + 1) * 2 * K + 2 * (q + 1))
                x1_squares(b, 2, lambda o: after_x1(b, 1, o))
                x_sums_next(1, 0, lambda o: after_x(b + 1, 1, o))
                x1_squares(b, 3, lambda o: after_x1(b, 2, o))
                u_sums(b, 0, u_freed(0), skip_top=1)
                x_sums_next(1, 1, lambda o: after_u(b, 0, 0))
                with act.Fori(2, K // 2) as j:
                    for q in range(2):
                        k = 2 * j + q
                        if not last:
                            load_stat(b + 1, k, q, (b + 1) * 2 * K + 2 * (k - 1))
                        x1_squares(b, k, lambda o: after_u(b, k - 4, 1))
                        u_sums(b, k - 3, u_freed(k - 3))
                        x_sums_next(j, q, lambda o: after_u(b, k - 3, 0))
                u_sums(b, K - 3, lambda o: after_x(b + 1, K - 1, 1) if o == 0 and not last
                       else after_u(b, K - 4, o))
                u_sums(b, K - 2, lambda o: after_u(b, K - 3, o))
                act.wait_ge(a_chain, after(A_STEPS, b, "att"))
                nc.scalar.activation(attn[:], ps_at, ACT.Sigmoid).then_inc(a_chain, 1)
                act.wait_ge(u_chain, after(U_STEPS, b, "corner"))
                after_u(b, K - 2, 1)
                for o in range(HALVES):
                    top = rows(o, 0, 1)
                    left_right = body[:, o, 1:H - ROWS, 1:W + 1:W - 1]
                    for n, (src, r, w) in enumerate(((top, 1, W), (left_right, H - ROWS - 1, 2))):
                        for m, func in enumerate((ACT.Identity, ACT.Square)):
                            dst = unused[:, 2 * n + m, o * 2 * W:o * 2 * W + r * w]
                            made = nc.scalar.activation(dst.rearrange("p (r w) -> p r w", w=w), src, func,
                                                        bias=u_neg_pivot[:, o:o + 1],
                                                        accum_out=u_part[:, 2 * m + o, K + n:K + n + 1])
                made.then_inc(edge_summed, 1)
                act.wait_ge(edge_summed, b + 1)
                for o in range(HALVES):
                    act.wait_ge(u_chain, after(U_STEPS, b, f"corner{o}"))
                    for m, func in enumerate((ACT.Identity, ACT.Square)):
                        made = nc.scalar.activation(grid(unused[:, 2 * o + m]), rows(o, H - ROWS, ROWS),
                                                    func, bias=u_neg_pivot[:, o:o + 1],
                                                    accum_out=u_part[:, 2 * m + o, K - 1:K])
                    made.then_inc(u_summed, 1)

            def relu_u(b, k, o):
                nc.scalar.activation(grid(ps_dw[:, o]), rows(o, k * ROWS, ROWS), ACT.Relu,
                                     bias=relu_shift[:, o:o + 1], scale=relu_scale[:, o:o + 1]
                                     ).then_inc(relu_done, 1)

            def write_h(b, k, o):
                act.wait_ge(conv1_done, b * 2 * K + 2 * k + o + 1)
                nc.scalar.activation(rows(o, k * ROWS + 1, ROWS), grid(ps_conv[:, o]), ACT.Relu,
                                     bias=bias1[:, o:o + 1]).then_inc(h_written, 1)

            def final_phase(b, conv1):
                def h_over_u(k):
                    for o in range(HALVES):
                        act.wait_ge(leaky_done, b * 2 * K + 2 * min_chunk(k) + o + 1)
                        write_h(b + 1, k, o)

                def min_chunk(k):
                    return k if isinstance(k, int) and k == K - 1 else k + 1

                def chunk(k, q):
                    for o in range(HALVES):
                        act.wait_ge(out_ready, b * 2 * K + 2 * k + o + 1)
                        relu_u(b, k + 1, o)
                    for o in range(HALVES):
                        store_out(b, k, q, o)
                    if conv1:
                        h_over_u(k)

                act.wait_ge(u_chain, after(U_STEPS, b, "rshift"))
                for o in range(HALVES):
                    relu_u(b, 0, o)
                with act.Fori(0, K // 2 - 1) as j:
                    for q in range(2):
                        chunk(2 * j + q, q)
                chunk(K - 2, 0)
                if conv1:
                    h_over_u(K - 1)
                for o in range(HALVES):
                    store_out(b, K - 1, 1, o)

            act.wait_ge(const_dve, CONST_CLEARED)
            for q in range(2):
                load_stat(0, q, q)
            x_sums(0, 0, 0)
            x_sums(0, 0, 1, lambda o: after_x(0, 0, o))
            with act.Fori(1, K // 2) as j:
                for q in range(2):
                    load_stat(0, 2 * j + q, q, 2 * (2 * j + q - 1))
                for q in range(2):
                    x_sums(0, j, q, lambda o: after_x(0, 2 * j + q - 1, o))
            with act.Fori(0, K) as k:
                for o in range(HALVES):
                    write_h(0, k, o)
            with act.Fori(0, B - 1) as b:
                conv2_phase(b, False)
                final_phase(b, True)
            conv2_phase(B - 1, True)
            final_phase(B - 1, False)
            for n in range(4):
                act.wait_ge(out_stored[n], 16 * B * (K // 2))

        @block.vector
        def _(dve):
            V = nc.vector

            def step(chain, steps, n, name, make):
                at = steps.index(name)
                if not (at == 0):
                    dve.wait_ge(chain, n * len(steps) + at)
                make().then_inc(chain, 1)

            def g_steps_to_mean(n):
                s = lambda name, make: step(g_chain, G_STEPS, n, name, make)
                s("total", lambda: V.reduce_sum(total[:], part[:], AX_X))
                s("dm", lambda: V.scalar_tensor_tensor(out=dm[:], in0=total[:, 0:4], scalar=1.0 / NPIX,
                                                       in1=neg_pivot[:], op0=ALU.mult, op1=ALU.add))
                s("dm2", lambda: V.tensor_tensor(tmp4[:], dm[:], dm[:], ALU.mult))
                s("var", lambda: V.scalar_tensor_tensor(out=var[:], in0=total[:, 4:8], scalar=1.0 / NPIX,
                                                        in1=tmp4[:], op0=ALU.mult, op1=ALU.subtract))
                s("var0", lambda: V.tensor_scalar(var[:], var[:], 0.0, None, ALU.max))
                s("mean", lambda: V.scalar_tensor_tensor(out=mean[:], in0=total[:, 0:4],
                                                         scalar=1.0 / NPIX, in1=add_back[:],
                                                         op0=ALU.mult, op1=ALU.add))

            def g_steps_to_q(n):
                s = lambda name, make: step(g_chain, G_STEPS, n, name, make)
                s("gmean", lambda: V.tensor_copy(gmean[:], ps_gm))
                s("dev", lambda: V.tensor_tensor(dev[:], mean[:], gmean[:], ALU.subtract))
                s("dev2", lambda: V.tensor_tensor(tmp4[:], dev[:], dev[:], ALU.mult))
                s("q", lambda: V.tensor_tensor(tmp4[:], tmp4[:], var[:], ALU.add))

            def g_steps_to_ve(n):
                step(g_chain, G_STEPS, n, "ve", lambda: V.tensor_scalar(tmp4[:], ps_gq, EPS, None, ALU.add))

            def x_steps_to_weights(n):
                s = lambda name, make: step(x_chain, X_STEPS, n, name, make)
                dve.wait_ge(g_chain, after(G_STEPS, n, "rstd"))
                s("t", lambda: V.tensor_tensor(xs_[:], var[:, 0:2], grstd[:, 0:2], ALU.mult))
                s("t2", lambda: V.tensor_tensor(xs_[:], xs_[:], grstd[:, 0:2], ALU.mult))
                s("te", lambda: V.tensor_scalar(xs_[:], xs_[:], EPS, None, ALU.add))
                dve.wait_ge(x_chain, after(X_STEPS, n, "rstd"))
                V.tensor_tensor(xs_[:], xr[:], grstd[:, 0:2], ALU.mult).then_inc(x_chain, 1)
                for i in range(HALVES):
                    s(f"w{i}", lambda i=i: V.tensor_scalar(w1_s[:, i, :], w1_raw[:, i, :],
                                                           xs_[:, i:i + 1], None, ALU.mult))

            def x_steps_to_bias(n):
                s = lambda name, make: step(x_chain, X_STEPS, n, name, make)
                s("bias", lambda: V.tensor_tensor(bias1[:], b1c, ps_b1, ALU.subtract))
                s("pivots", lambda: V.tensor_scalar(neg_pivot[:, 2:4], mean[:, 0:2], -1.0, None, ALU.mult))

            def u_pivot_step(n):
                s = lambda name, make: step(x_chain, X_STEPS, n, name, make)
                s("upivot", lambda: V.tensor_tensor(u_neg_pivot[:], neg_pivot[:, 2:4], tap_sum[:], ALU.mult))

            def h_steps(b):
                s = lambda name, make: step(h_chain, H_STEPS, b, name, make)
                dve.wait_ge(h_counted, (b + 1) * 2 * K)
                s("top", lambda: V.memset(body[:, :, 0, :], 0.0))
                for i in range(HALVES):
                    V.bn_aggr(h_mv[:, i, :], h_stats[:, i].rearrange("p a b -> p (a b)")
                              ).then_inc(h_chain, 1)
                s("ve", lambda: V.tensor_scalar(h_ve[:], h_mv[:, :, 1], EPS, None, ALU.add))
                for i in range(HALVES):
                    s(f"w{i}", lambda i=i: V.tensor_scalar(w2_s[:, i, :], w2_raw[:, i, :],
                                                           h_rstd[:, i:i + 1], None, ALU.mult))
                s("neg", lambda: V.tensor_tensor(neg_beta2[:], ps_b2, b2c, ALU.subtract))
                s("beta", lambda: V.tensor_scalar(beta2[:], neg_beta2[:], -1.0, None, ALU.mult))
                dve.wait_ge(h_chain, after(H_STEPS, b, "beta"))
                V.tensor_copy(add_back[:, 2:4], beta2[:])

            def write_x1(b, j, q):
                k = 2 * j + q
                dve.wait_ge(conv2_done, b * K + k + 1)
                dve.wait_ge(x_loaded[q], 16 * (b * K + K // 2 + j + 1))
                for o in range(HALVES):
                    V.scalar_tensor_tensor(out=rows(o, k * ROWS + 1, ROWS), in0=grid(ps_conv[:, o]),
                                           scalar=neg_beta2[:, o:o + 1], in1=grid(x_ring[:, q, o]),
                                           op0=ALU.max, op1=ALU.add,
                                           accum_out=part[:, 2 + o, bass.ds(k, 1)]).then_inc(x1_half, 1)

            def write_u(b, k, j, q, o):
                dve.wait_ge(dw_products, b * 2 * K + 2 * k + o + 1)
                dve.wait_ge(x1_squared, b * 2 * K + 2 * k + o + 1)
                dve.wait_ge(spilled[q], 32 * (b * (K // 2) + j + 1))
                before = o * (NT[0] - 1)
                for m, t in enumerate(DVE_TAPS[o]):
                    dy, dx = TAPS[t]
                    final = m == NT[o] - 1
                    if m > 0:
                        dve.wait_ge(tap_added, (b * K + k) * (NT[0] + NT[1] - 2) + before + m)
                    ins = V.scalar_tensor_tensor(
                        out=rows(o, k * ROWS, ROWS) if final else grid(ps_dw[:, o]),
                        in0=rows(o, k * ROWS + 1 + dy, ROWS, 1 + dx), scalar=taps[:, o, t:t + 1],
                        in1=grid(ps_dw[:, o]), op0=ALU.mult, op1=ALU.add)
                    ins.then_inc(u_written if final else tap_added, 1)

            def hidden_steps(b):
                s = lambda name, make: step(a_chain, A_STEPS, b, name, make)
                s("copy", lambda: V.tensor_copy(hidden_raw[:], ps_hid))
                s("leaky", lambda: V.scalar_tensor_tensor(out=hidden[:], in0=hidden_raw[:], scalar=SLOPE,
                                                          in1=hidden_raw[:], op0=ALU.mult, op1=ALU.max))

            def a_steps_to_end(b):
                s = lambda name, make: step(a_chain, A_STEPS, b, name, make)
                s("alpha", lambda: V.tensor_tensor(alpha[:], attn[:], grstd[:, 2:4], ALU.mult))
                s("k", lambda: V.tensor_tensor(padk[:], gmean[:, 2:4], beta2[:], ALU.subtract))
                wide = padk[:].unsqueeze(2).to_broadcast([P, HALVES, 2])
                s("krows", lambda: V.tensor_tensor(k_rows[:], edge_rows[:], wide, ALU.mult))
                s("kcols", lambda: V.tensor_tensor(k_cols[:], edge_cols[:], wide, ALU.mult))
                corners = taps[:].rearrange("p o (y x) -> p o y x", x=3)[:, :, 0:3:2, 0:3:2]
                s("kcorner", lambda: V.tensor_tensor(
                    k_corner[:], corners,
                    padk[:].unsqueeze(2).unsqueeze(3).to_broadcast([P, HALVES, 2, 2]), ALU.mult))
                s("kw", lambda: V.tensor_tensor(v(5), padk[:], tap_sum[:], ALU.mult))
                s("akw", lambda: V.tensor_tensor(v(5), v(5), alpha[:], ALU.mult))
                s("c0", lambda: V.tensor_tensor(v(5), rbc, v(5), ALU.subtract))

            def v(i):
                return uv[:, i, :]

            def edge_steps(b):
                s = lambda name, make: step(u_chain, U_STEPS, b, name, make)
                dve.wait_ge(a_chain, after(A_STEPS, b, "c0"))
                dve.wait_ge(u_summed, b * 2 * K + 2 * (K - 1))
                t = body[:, :, 0, 1:W + 1]
                s("top", lambda: V.tensor_tensor(t, t, k_rows[:, :, 0:1].to_broadcast([P, HALVES, W]), ALU.add))
                n = H - ROWS
                lr = body[:, :, 0:n, 1:W + 1:W - 1]
                s("cols", lambda: V.tensor_tensor(lr, lr, k_cols[:].unsqueeze(2).to_broadcast([P, HALVES, n, 2]), ALU.add))
                c = body[:, :, 0, 1:W + 1:W - 1]
                s("corner", lambda: V.tensor_tensor(c, c, k_corner[:, :, 0, :], ALU.subtract))

            def last_edge_steps(b, o):
                s = lambda name, make: step(u_chain, U_STEPS, b, name, make)
                r = body[:, o, H - 1, 1:W + 1]
                dve.wait_ge(u_written, b * 2 * K + 2 * (K - 1) + o + 1)
                s(f"bottom{o}", lambda: V.tensor_scalar(r, r, k_rows[:, o, 1:2], None, ALU.add))
                lr = body[:, o, H - ROWS:H, 1:W + 1:W - 1]
                s(f"cols{o}", lambda: V.tensor_tensor(lr, lr, k_cols[:, o:o + 1, :].to_broadcast([P, ROWS, 2]), ALU.add))
                c = body[:, o, H - 1, 1:W + 1:W - 1]
                s(f"corner{o}", lambda: V.tensor_tensor(c, c, k_corner[:, o, 1, :], ALU.subtract))

            def u_steps(b):
                s = lambda name, make: step(u_chain, U_STEPS, b, name, make)
                side = lambda name, make: step(m_chain, M_STEPS, b, name, make)
                dve.wait_ge(u_summed, (b + 1) * 2 * K)
                s("total", lambda: V.reduce_sum(u_total[:], u_part[:], AX_X))
                s("m", lambda: V.tensor_scalar(v(0), u_total[:, 0:2], 1.0 / NPIX, None, ALU.mult))
                s("m2", lambda: V.tensor_tensor(v(1), v(0), v(0), ALU.mult))
                s("var", lambda: V.scalar_tensor_tensor(out=v(1), in0=u_total[:, 2:4], scalar=1.0 / NPIX,
                                                        in1=v(1), op0=ALU.mult, op1=ALU.subtract))
                s("vt", lambda: V.scalar_tensor_tensor(out=v(3), in0=v(1), scalar=0.0, in1=alpha[:],
                                                       op0=ALU.max, op1=ALU.mult))
                s("vt2", lambda: V.tensor_tensor(v(3), v(3), alpha[:], ALU.mult))
                s("te", lambda: V.tensor_scalar(v(3), v(3), EPS, None, ALU.add))
                side("mean", lambda: V.tensor_tensor(v(0), v(0), u_neg_pivot[:], ALU.subtract))
                side("am", lambda: V.tensor_tensor(v(6), alpha[:], v(0), ALU.mult))
                side("mu", lambda: V.tensor_tensor(v(6), v(6), v(5), ALU.add))
                side("d", lambda: V.tensor_tensor(v(7), v(5), v(6), ALU.subtract))
                dve.wait_ge(m_chain, after(M_STEPS, b, "d"))
                s("rscale", lambda: V.scalar_tensor_tensor(out=relu_scale[:], in0=alpha[:], scalar=1.0 - SLOPE,
                                                           in1=v(4), op0=ALU.mult, op1=ALU.mult))
                s("rshift", lambda: V.scalar_tensor_tensor(out=relu_shift[:], in0=v(7), scalar=1.0 - SLOPE,
                                                           in1=v(4), op0=ALU.mult, op1=ALU.mult))
                s("sscale", lambda: V.scalar_tensor_tensor(out=slope_scale[:], in0=alpha[:], scalar=SLOPE,
                                                           in1=v(4), op0=ALU.mult, op1=ALU.mult))
                s("oshift", lambda: V.scalar_tensor_tensor(out=v(2), in0=v(7), scalar=SLOPE,
                                                           in1=v(4), op0=ALU.mult, op1=ALU.mult))
                s("last", lambda: V.tensor_tensor(out_shift[:], v(2), beta2[:], ALU.add))

            def conv2_phase(b, last):
                write_x1(b, 0, 0)
                write_x1(b, 0, 1)
                write_x1(b, 1, 0)
                write_u(b, 0, 0, 0, 0)
                write_u(b, 0, 0, 0, 1)
                write_x1(b, 1, 1)
                write_u(b, 1, 0, 1, 0)
                write_u(b, 1, 0, 1, 1)
                with dve.Fori(2, K // 2) as j:
                    for q in range(2):
                        write_x1(b, j, q)
                        for o in range(HALVES):
                            write_u(b, 2 * j + q - 2, j - 1, q, o)
                dve.wait_ge(x1_squared, (b + 1) * 2 * K)
                dve.wait_ge(x_summed, (b + 2) * 2 * K if not last else B * 2 * K)
                g_steps_to_mean(b + 1)
                g_steps_to_q(b + 1)
                g_steps_to_ve(b + 1)
                write_u(b, K - 2, K // 2 - 1, 0, 0)
                dve.wait_ge(g_chain, after(G_STEPS, b + 1, "rstd"))
                step(a_chain, A_STEPS, b, "pool",
                     lambda: V.tensor_tensor(pooled[:], dev[:, 2:4], grstd[:, 2:4], ALU.mult))
                if not last:
                    x_steps_to_weights(b + 1)
                write_u(b, K - 2, K // 2 - 1, 0, 1)
                hidden_steps(b)
                if not last:
                    x_steps_to_bias(b + 1)
                write_u(b, K - 1, K // 2 - 1, 1, 0)
                a_steps_to_end(b)
                edge_steps(b)
                last_edge_steps(b, 0)
                write_u(b, K - 1, K // 2 - 1, 1, 1)
                last_edge_steps(b, 1)
                u_steps(b)
                if not last:
                    u_pivot_step(b + 1)

            def make_out(b, j, q):
                at = b * 2 * K + 4 * j + 2 * q
                for o in range(HALVES):
                    dve.wait_ge(relu_done, at + o + 1)
                    V.scalar_tensor_tensor(out=grid(ps_dw[:, o]), in0=rows(o, (2 * j + q) * ROWS, ROWS),
                                           scalar=slope_scale[:, o:o + 1], in1=grid(ps_dw[:, o]),
                                           op0=ALU.mult, op1=ALU.add).then_inc(leaky_done, 1)
                for o in range(HALVES):
                    dve.wait_ge(fin_loaded[2 * q + o], 16 * (b * (K // 2) + j + 1))
                    dve.wait_ge(leaky_done, at + o + 1)
                    V.scalar_tensor_tensor(out=fin_ring[:, q, o], in0=ps_dw[:, o],
                                           scalar=out_shift[:, o:o + 1], in1=fin_ring[:, q, o],
                                           op0=ALU.add, op1=ALU.add).then_inc(out_ready, 1)

            def count_h(b, j, q):
                for o in range(HALVES):
                    dve.wait_ge(h_written, b * 2 * K + 4 * j + 2 * q + o + 1)
                    for n in range(2):
                        k2 = 4 * j + 2 * q + n
                        ins = V.bn_stats(h_stats[:, o, bass.ds(k2, 1), :].rearrange("p a b -> p (a b)"),
                                         rows(o, 2 * (2 * j + q) * BROWS + 1 + n * BROWS, BROWS))
                    ins.then_inc(h_counted, 1)

            V.memset(part[:], 0.0).then_inc(const_dve, 1)
            V.memset(neg_pivot[:, 2:4], 0.0).then_inc(const_dve, 1)
            V.memset(add_back[:], 0.0).then_inc(const_dve, 1)
            V.memset(body[:], 0.0).then_inc(const_dve, 1)
            dve.wait_ge(const_loaded, 16 * 8)
            dve.wait_ge(const_pool, 6)
            for o in range(HALVES):
                for m, t in enumerate(PE_TAPS[o]):
                    V.tensor_scalar(diag[:, o, m, :], ident[:], taps[:, o, t:t + 1], None, ALU.mult
                                    ).then_inc(const_dve, 1)
            V.reduce_sum(edge_rows[:], taps[:].rearrange("p o (y x) -> p o y x", x=3)[:, :, 0:3:2, :],
                         AX_X).then_inc(const_dve, 1)
            V.reduce_sum(edge_cols[:], taps[:].rearrange("p o (y x) -> p o x y", x=3)[:, :, 0:3:2, :],
                         AX_X).then_inc(const_dve, 1)
            V.reduce_sum(tap_sum[:], taps[:], AX_X).then_inc(const_dve, 1)

            dve.wait_ge(const_dve, CONST_DVE)
            dve.wait_ge(x_summed, 2 * K)
            g_steps_to_mean(0)
            g_steps_to_q(0)
            g_steps_to_ve(0)
            x_steps_to_weights(0)
            x_steps_to_bias(0)
            u_pivot_step(0)
            with dve.Fori(0, K // 2) as j:
                for q in range(2):
                    count_h(0, j, q)
            h_steps(0)
            with dve.Fori(0, B - 1) as b:
                conv2_phase(b, False)
                make_out(b, 0, 0)
                make_out(b, 0, 1)
                count_h(b + 1, 0, 0)
                with dve.Fori(1, K // 2) as j:
                    for q in range(2):
                        make_out(b, j, q)
                        count_h(b + 1, j - 1 + q, 1 - q)
                count_h(b + 1, K // 2 - 1, 1)
                h_steps(b + 1)
            conv2_phase(B - 1, True)
            with dve.Fori(0, K // 2) as j:
                for q in range(2):
                    make_out(B - 1, j, q)


def kernel(**inputs):
    import numpy as np
    import concourse.bacc as bacc
    from concourse.bass_utils import run_bass_kernel_spmd

    C = inputs["x"].shape[1]
    column = lambda a: np.ascontiguousarray(np.asarray(a).reshape(2, C // 2).T)
    arrays = {
        "x": np.ascontiguousarray(inputs["x"]),
        "w1t": np.ascontiguousarray(np.asarray(inputs["L0_conv_w1"]).T),
        "b1": column(inputs["L0_conv_b1"]),
        "w2t": np.ascontiguousarray(np.asarray(inputs["L0_conv_w2"]).T),
        "b2": column(inputs["L0_conv_b2"]),
        "a1t": np.ascontiguousarray(np.asarray(inputs["L1_conv_attn_w1"]).T),
        "a2t": np.ascontiguousarray(np.asarray(inputs["L1_conv_attn_w2"]).T),
        "rw": np.ascontiguousarray(np.asarray(inputs["L1_conv_refine_w"]).reshape(C, 9)),
        "rb": column(inputs["L1_conv_refine_b"]),
    }
    nc = bacc.Bacc("TRN2", target_bir_lowering=False, num_devices=1)
    aps = [nc.dram_tensor(f"in_{n}", a.shape, mybir.dt.from_np(a.dtype), kind="ExternalInput").ap()
           for n, a in arrays.items()]
    out = nc.dram_tensor("out_0", inputs["x"].shape, F32, kind="ExternalOutput").ap()
    conv_preact_kernel(nc, *aps, out)
    r = run_bass_kernel_spmd(nc, [{f"in_{n}": a for n, a in arrays.items()}], core_ids=[0])
    return r.results[0]["out_0"]
```

```python
from contextlib import ExitStack

import concourse.bass as bass
from concourse import mybir

ALU = mybir.AluOpType
ACT = mybir.ActivationFunctionType
F32 = mybir.dt.float32
AX_X = mybir.AxisListType.X

P = 128
EPS = 1e-5
SLOPE = 0.01
TAPS = [(dy, dx) for dy in (-1, 0, 1) for dx in (-1, 0, 1)]
SUMMED_TAPS = [[0, 2, 6], [0, 2, 6, 8]]
OTHER_TAPS = [[4, 1, 7, 3, 5, 8], [4, 1, 7, 3, 5]]
TENSOR_TAPS = [(2, 2), (3, 2)]
TAIL_TENSOR_TAPS = [[(4, 4), (4, 4)], [(3, 3), (3, 3)], [(4, 4), (4, 4)]]
TAIL_SUMMED = [[3, 4], [3, 3], [2, 3]]
MOST_TENSOR_TAPS = 4


def vector_taps(half, division, summed):
    first, second = division
    taps = OTHER_TAPS[half]
    return ([(t, 1) for t in taps[second:first]] + [(t, None) for t in taps[first:]]
            + [(t, None) for t in SUMMED_TAPS[half][summed:]])


def conv_preact_kernel(nc, x, w1t, b1, w2t, b2, a1t, a2t, rw, rb, out):
    B, C, H, W = x.shape
    HALVES = C // P
    HID = a1t.shape[1]
    GROUP = C // 32
    ROWS = 8
    CP = ROWS * W
    K = H // ROWS
    BANK = 512
    BROWS = BANK // W
    NPIX = H * W
    PITCH = W + 2
    TAIL = len(TAIL_SUMMED)
    assert H == W and HALVES == 2 and CP == 2 * BANK and K % 2 == 0

    xv = x.rearrange("b (o p) h w -> p (b o) (h w)", p=P)
    ov = out.rearrange("b (o p) h w -> p (b o) (h w)", p=P)
    x1_dram = nc.dram_tensor("x1_dram", [B, C, NPIX], F32, kind="Internal").ap()
    x1v = x1_dram.rearrange("b (o p) n -> p (b o) n", p=P)

    with ExitStack() as ctx:
        def sb(name, shape):
            return ctx.enter_context(nc.sbuf_tensor(name, shape, F32))

        def sem(name):
            return ctx.enter_context(nc.semaphore(name))

        body = sb("body", [P, HALVES, H + 2, PITCH])
        x_ring = sb("x_ring", [P, 2, HALVES, CP])
        stat_ring = sb("stat_ring", [P, 2, HALVES, CP])
        fin_ring = sb("fin_ring", [P, 2, HALVES, CP])
        tap_part = [fin_ring[:, o, 0] for o in range(HALVES)]
        tap_product = [fin_ring[:, o, 1] for o in range(HALVES)]
        unused = ctx.enter_context(nc.sbuf_tensor("unused", [P, 4, CP], mybir.dt.bfloat16))
        w1_raw = sb("w1_raw", [P, HALVES, C])
        w2_raw = sb("w2_raw", [P, HALVES, C])
        w1_s = sb("w1_s", [P, HALVES, C])
        w2_s = sb("w2_s", [P, HALVES, C])
        att1 = sb("att1", [P, HALVES, HID])
        att2 = sb("att2", [HID, C])
        taps = sb("taps", [P, HALVES, 9])
        vecs = sb("vecs", [P, 3, HALVES])
        b1c, b2c, rbc = (vecs[:, i, :] for i in range(3))
        ident = sb("ident", [P, P])
        group = sb("group", [P, P])
        diag = sb("diag", [P, HALVES, MOST_TENSOR_TAPS, P])
        minus_half = sb("minus_half", [P, 4])
        tap_sum = sb("tap_sum", [P, HALVES])
        edge_rows = sb("edge_rows", [P, HALVES, 2])
        edge_cols = sb("edge_cols", [P, HALVES, 2])
        edge_weight = sb("edge_weight", [P, HALVES])
        corner_sum = sb("corner_sum", [P, HALVES])
        part = sb("part", [P, 8, K])
        total = sb("total", [P, 8])
        u_part = sb("u_part", [P, 4, K + 2])
        u_total = sb("u_total", [P, 4])
        x_stats = sb("x_stats", [P, 2 * K, 6])
        x_mv = sb("x_mv", [P, 2])
        h_stats = sb("h_stats", [P, HALVES, 2 * K, 6])
        h_mv = sb("h_mv", [P, HALVES, 2])
        h_ve = sb("h_ve", [P, HALVES])
        h_rstd = sb("h_rstd", [P, HALVES])
        beta2 = sb("beta2", [P, HALVES])
        neg_beta2 = sb("neg_beta2", [P, HALVES])
        bias1 = sb("bias1", [P, HALVES])
        neg_pivot = sb("neg_pivot", [P, 4])
        add_back = sb("add_back", [P, 4])
        dm = sb("dm", [P, 4])
        var = sb("var", [P, 4])
        mean = sb("mean", [P, 4])
        gmean = sb("gmean", [P, 4])
        dev = sb("dev", [P, 4])
        tmp4 = sb("tmp4", [P, 4])
        grstd = sb("grstd", [P, 4])
        xs_ = sb("xs_", [P, HALVES])
        xr = sb("xr", [P, HALVES])
        pooled = sb("pooled", [P, HALVES])
        hidden_raw = sb("hidden_raw", [HID, 1])
        hidden = sb("hidden", [HID, 1])
        attn = sb("attn", [P, HALVES])
        alpha = sb("alpha", [P, HALVES])
        padk = sb("padk", [P, HALVES])
        u_neg_pivot = sb("u_neg_pivot", [P, HALVES])
        k_rows = sb("k_rows", [P, HALVES, 2])
        k_cols = sb("k_cols", [P, HALVES, 2])
        k_corner = sb("k_corner", [P, HALVES, 2, 2])
        uv = sb("uv", [P, 8, HALVES])
        relu_scale = sb("relu_scale", [P, HALVES])
        relu_shift = sb("relu_shift", [P, HALVES])
        slope_scale = sb("slope_scale", [P, HALVES])
        out_shift = sb("out_shift", [P, HALVES])

        ps_conv = ctx.enter_context(nc.psum_tensor("ps_conv", [P, HALVES, CP], F32))
        ps_dw = ctx.enter_context(nc.psum_tensor("ps_dw", [P, HALVES, CP], F32))
        ps_gm, ps_gq = ps_conv[:, 0, 0:4], ps_conv[:, 0, 4:8]
        ps_b1 = ps_conv[:, 0, BANK:BANK + 2]
        ps_hid = ps_conv[0:HID, 1, 0:1]
        ps_at = ps_conv[:, 1, BANK:BANK + 2]
        ps_b2 = ps_conv[:, 1, BANK:BANK + 2]

        const_loaded = sem("const_loaded")
        const_pool = sem("const_pool")
        const_dve = sem("const_dve")
        x_loaded = [sem(f"x_loaded{q}") for q in range(2)]
        stat_loaded = [sem(f"stat_loaded{q}") for q in range(2)]
        fin_loaded = [sem(f"fin_loaded{n}") for n in range(4)]
        out_stored = [sem(f"out_stored{n}") for n in range(4)]
        spilled = [sem(f"spilled{q}") for q in range(2)]
        conv1_done = sem("conv1_done")
        h_written = sem("h_written")
        conv2_done = sem("conv2_done")
        x1_half = sem("x1_half")
        x1_squared = sem("x1_squared")
        dw_products = sem("dw_products")
        tap_multiplied = sem("tap_multiplied")
        tap_summed = sem("tap_summed")
        tap_added = sem("tap_added")
        u_written = sem("u_written")
        u_summed = sem("u_summed")
        x_pivot = sem("x_pivot")
        x_summed = sem("x_summed")
        x_counted = sem("x_counted")
        relu_done = sem("relu_done")
        leaky_done = sem("leaky_done")
        out_ready = sem("out_ready")
        h_counted = sem("h_counted")
        h_chain = sem("h_chain")
        g_chain = sem("g_chain")
        x_chain = sem("x_chain")
        a_chain = sem("a_chain")
        k_chain = sem("k_chain")
        u_chain = sem("u_chain")
        edge_summed = sem("edge_summed")
        m_chain = sem("m_chain")

        H_STEPS = ["top", "aggr0", "aggr1", "ve", "rstd", "w0", "w1", "prod", "neg", "beta",
                   "back"]
        G_STEPS = ["total", "aggr", "dm", "dm2", "var", "var0", "mean", "mean1",
                   "var1", "prod", "gmean", "dev", "dev2",
                   "q", "prod2", "ve", "rstd"]
        X_STEPS = ["t", "t2", "te", "rstd", "s", "w0", "w1", "prod", "bias", "pivots", "upivot"]
        K_STEPS = ["k", "krows", "kcols", "kcorner", "ksum", "kpivot", "kw"]
        A_STEPS = ["pool", "hid", "copy", "leaky", "att", "sigmoid", "alpha", "akw", "c0"]
        U_STEPS = ["top", "cols", "corner", "bottom0", "cols0", "corner0", "bottom1", "cols1",
                   "corner1", "total", "m", "m2", "var", "vt", "vt2", "te", "rstd", "rscale", "rshift",
                   "sscale", "oshift", "last"]
        M_STEPS = ["mean", "am", "mu", "d"]

        CONST_CLEARED = 5
        CONST_DVE = CONST_CLEARED + HALVES * MOST_TENSOR_TAPS + 6

        def after(steps, n, name):
            return n * len(steps) + steps.index(name) + 1

        def division(k, o):
            return TAIL_TENSOR_TAPS[k - (K - TAIL)][o] if isinstance(k, int) and k >= K - TAIL else TENSOR_TAPS[o]

        def summed(k, o):
            return TAIL_SUMMED[k - (K - TAIL)][o] if isinstance(k, int) and k >= K - TAIL else len(SUMMED_TAPS[o])

        def count_before(steps, b, k, o):
            each = steps(0, 0) + steps(0, 1)
            tail = [steps(K - TAIL + i, o) for i in range(TAIL) for o in range(HALVES)]
            whole = (K - TAIL) * each + sum(tail)
            if isinstance(k, int) and k >= K - TAIL:
                return b * whole + (K - TAIL) * each + sum(tail[:(k - (K - TAIL)) * HALVES + o])
            return b * whole + k * each + o * steps(0, 0)

        def taps_before(b, k, o):
            return count_before(lambda k, o: len(vector_taps(o, division(k, o), summed(k, o))), b, k, o)

        def products_before(b, k, o):
            return count_before(summed, b, k, o)

        def sums_before(b, k, o):
            return count_before(lambda k, o: summed(k, o) - 1, b, k, o)

        def rows(o, first, count, c0=1, cn=W):
            return body[:, o, bass.ds(first, count), c0:c0 + cn]

        def grid(ap):
            return ap.rearrange("p (r w) -> p r w", w=W)

        block = ctx.enter_context(nc.Block())

        @block.sync
        def _(sp):
            for dst, src in ((w1_raw[:], w1t.rearrange("(o p) n -> p o n", p=P)),
                             (w2_raw[:], w2t.rearrange("(o p) n -> p o n", p=P)),
                             (att1[:], a1t.rearrange("(o p) n -> p o n", p=P)),
                             (att2[:], a2t),
                             (taps[:], rw.rearrange("(o p) t -> p o t", p=P)),
                             (b1c, b1), (b2c, b2), (rbc, rb)):
                sp.dma_start(dst, src).then_inc(const_loaded, 16)

            def load_x(b, k, q):
                sp.dma_start(x_ring[:, q], xv[:, bass.ds(b * HALVES, HALVES), bass.ds(k * CP, CP)]
                             ).then_inc(x_loaded[q], 16)

            def load_fin(b, k, q):
                for o in range(HALVES):
                    sp.dma_start(fin_ring[:, q, o:o + 1],
                                 x1v[:, bass.ds(b * HALVES + o, 1), bass.ds(k * CP, CP)]
                                 ).then_inc(fin_loaded[2 * q + o], 16)

            def reload_fin(b, k, j, q):
                for o in range(HALVES):
                    sp.wait_ge(out_stored[2 * q + o], 16 * (b * (K // 2) + j))
                load_fin(b, k, q)

            def conv1_streams(b, final):
                if final:
                    for q in range(2):
                        reload_fin(b - 1, 2 + q, 1, q)
                with sp.Fori(2, K // 2) as j:
                    for q in range(2):
                        k = 2 * j + q
                        sp.wait_ge(conv1_done, b * 2 * K + 2 * (k - 1))
                        load_x(b, k, q)
                        if final:
                            reload_fin(b - 1, k, j, q)
                for q in range(2):
                    sp.wait_ge(conv1_done, b * 2 * K + 2 * (K - 1 + q))
                    if final and q == 1:
                        for o in range(HALVES):
                            sp.wait_ge(out_ready, (b - 1) * 2 * K + 2 * K - 1 + o)
                            sp.dma_start(ov[:, bass.ds((b - 1) * HALVES + o, 1), (K - 1) * CP:K * CP],
                                         fin_ring[:, 1, o:o + 1]).then_inc(out_stored[2 + o], 16)
                        for n in range(4):
                            sp.wait_ge(out_stored[n], 16 * b * (K // 2))
                    load_x(b, q, q)

            def spill_x1(b, k, q):
                sp.wait_ge(x1_half, b * 2 * K + 2 * (k + 1))
                for o in range(HALVES):
                    sp.dma_start(x1v[:, bass.ds(b * HALVES + o, 1), bass.ds(k * CP, CP)]
                                 .rearrange("p a (r w) -> p (a r) w", w=W),
                                 rows(o, k * ROWS + 1, ROWS)).then_inc(spilled[q], 16)

            def conv2_streams(b, last):
                with sp.Fori(0, K // 2 - 1) as j:
                    for q in range(2):
                        k = 2 * j + q
                        spill_x1(b, k, q)
                        load_x(b, k + 2, q)
                for q in range(2):
                    spill_x1(b, K - 2 + q, q)
                    if not last:
                        load_x(b + 1, 2 + q, q)
                for q in range(2):
                    sp.wait_ge(tap_added, taps_before(b, K - 1, q) + 1)
                    sp.wait_ge(spilled[q], 32 * (b + 1) * (K // 2))
                    load_fin(b, q, q)

            for q in range(2):
                load_x(0, 2 + q, q)
            conv1_streams(0, False)
            conv2_streams(0, False)
            with sp.Fori(1, B - 1) as b:
                conv1_streams(b, True)
                conv2_streams(b, False)
            conv1_streams(B - 1, True)
            conv2_streams(B - 1, True)
            with sp.Fori(1, K // 2) as j:
                for q in range(2):
                    reload_fin(B - 1, 2 * j + q, j, q)

        @block.gpsimd
        def _(pool):
            nc.gpsimd.memset(ident[:], 0.0).then_inc(const_pool, 1)
            nc.gpsimd.memset(group[:], 1.0 / GROUP).then_inc(const_pool, 1)
            nc.gpsimd.memset(minus_half[:], -0.5).then_inc(const_pool, 1)
            pool.wait_ge(const_pool, 3)
            nc.gpsimd.affine_select(out=ident[:], in_=ident[:], compare_op=ALU.not_equal, fill=1.0,
                                    base=0, pattern=[[-1, P]], channel_multiplier=1
                                    ).then_inc(const_pool, 1)
            blocks = group[:].rearrange("p (g c) -> p g c", c=GROUP)
            nc.gpsimd.affine_select(out=blocks, in_=blocks, compare_op=ALU.is_ge, fill=0.0, base=0,
                                    pattern=[[-GROUP, P // GROUP], [0, GROUP]], channel_multiplier=1
                                    ).then_inc(const_pool, 1)
            pool.wait_ge(const_pool, 5)
            nc.gpsimd.affine_select(out=blocks, in_=blocks, compare_op=ALU.is_ge, fill=0.0,
                                    base=GROUP - 1, pattern=[[GROUP, P // GROUP], [0, GROUP]],
                                    channel_multiplier=-1).then_inc(const_pool, 1)

            def power(out_, in_, n):
                return nc.gpsimd.tensor_tensor(out_, in_, minus_half[:, 0:n], ALU.pow)

            def group_rsqrt(n):
                pool.wait_ge(g_chain, after(G_STEPS, n, "ve"))
                power(grstd[:], tmp4[:], 4).then_inc(g_chain, 1)

            def x_rsqrt(n):
                pool.wait_ge(x_chain, after(X_STEPS, n, "te"))
                power(xr[:], xs_[:], 2).then_inc(x_chain, 1)

            def u_rsqrt(b):
                pool.wait_ge(u_chain, after(U_STEPS, b, "te"))
                power(uv[:, 4, :], uv[:, 3, :], 2).then_inc(u_chain, 1)

            def h_rsqrt(b):
                pool.wait_ge(h_chain, after(H_STEPS, b, "ve"))
                power(h_rstd[:], h_ve[:], 2).then_inc(h_chain, 1)

            def sum_taps(b, k, o):
                for m in range(1, summed(k, o)):
                    pool.wait_ge(tap_multiplied, products_before(b, k, o) + m + 1)
                    if m > 1:
                        pool.wait_ge(tap_summed, sums_before(b, k, o) + m - 1)
                    nc.gpsimd.tensor_tensor(tap_part[o], tap_part[o], tap_product[o], ALU.add
                                            ).then_inc(tap_summed, 1)

            def conv2_phase(b, with_x):
                with pool.Fori(0, K - TAIL) as k:
                    for o in range(HALVES):
                        sum_taps(b, k, o)
                for k in range(K - TAIL, K - 1):
                    for o in range(HALVES):
                        sum_taps(b, k, o)
                group_rsqrt(b + 1)
                sum_taps(b, K - 1, 0)
                if with_x:
                    x_rsqrt(b + 1)
                sum_taps(b, K - 1, 1)
                u_rsqrt(b)

            group_rsqrt(0)
            x_rsqrt(0)
            h_rsqrt(0)
            with pool.Fori(0, B - 1) as b:
                conv2_phase(b, True)
                h_rsqrt(b + 1)
            conv2_phase(B - 1, False)

        @block.tensor
        def _(pe):
            def conv1_chunk(b, j, q):
                if isinstance(j, int) and j == 0:
                    chunk = stat_ring[:, 1 - q]
                else:
                    chunk = x_ring[:, q]
                    pe.wait_ge(x_loaded[q], 16 * (b * (K - 1) + j))
                for o in range(HALVES):
                    if not (isinstance(b, int) and isinstance(j, int) and b == 0 and j == 0 and q == 0):
                        pe.wait_ge(h_written, b * 2 * K + 4 * j + 2 * q + o - 1)
                    for n in range(2):
                        for i in range(HALVES):
                            mm = pe.matmul(ps_conv[:, o, n * BANK:(n + 1) * BANK],
                                           w1_s[:, i, o * P:(o + 1) * P],
                                           chunk[:, i, n * BANK:(n + 1) * BANK],
                                           start=i == 0, stop=i == HALVES - 1)
                    mm.then_inc(conv1_done, 1)

            def conv1_phase(b):
                pe.wait_ge(x_chain, after(X_STEPS, b, "bias"))
                if not isinstance(b, int):
                    pe.wait_ge(a_chain, after(A_STEPS, b - 1, "sigmoid"))
                for q in range(2):
                    conv1_chunk(b, 0, q)
                with pe.Fori(1, K // 2) as j:
                    for q in range(2):
                        conv1_chunk(b, j, q)

            def conv2_weights(b):
                pe.wait_ge(h_chain, after(H_STEPS, b, "w1"))
                for o in range(HALVES):
                    for i in range(HALVES):
                        mm = pe.matmul(ps_b2[:, o:o + 1], w2_s[:, i, o * P:(o + 1) * P],
                                       h_mv[:, i, 0:1], start=i == 0, stop=i == HALVES - 1)
                mm.then_inc(h_chain, 1)

            def conv2_chunk(b, k):
                ps = ps_dw if isinstance(k, int) and k == 1 else ps_conv
                for o in range(HALVES):
                    if isinstance(k, int) and k == 1:
                        pe.wait_ge(h_chain, after(H_STEPS, b, "back"))
                    elif isinstance(k, int) and k == 2:
                        pe.wait_ge(x1_half, b * 2 * K + o + 1)
                    elif isinstance(k, int) and k == 0:
                        if o == 1:
                            pe.wait_ge(h_chain, after(H_STEPS, b, "neg"))
                    else:
                        pe.wait_ge(x1_half, b * 2 * K + 2 * k + o - 1)
                    for n in range(2):
                        for i in range(HALVES):
                            mm = pe.matmul(ps[:, o, n * BANK:(n + 1) * BANK],
                                           w2_s[:, i, o * P:(o + 1) * P],
                                           rows(i, k * ROWS + 1 + n * BROWS, BROWS),
                                           start=i == 0, stop=i == HALVES - 1)
                mm.then_inc(conv2_done, 1)

            def dw_half(b, k, o, edge=None):
                pe.wait_ge(x1_half, b * 2 * K + 2 * (k + (1 if edge == "last" else 2)))
                if edge != "first":
                    pe.wait_ge(u_written, b * 2 * K + 2 * k + o - 1)
                for n in range(2):
                    mine = OTHER_TAPS[o][:division(k, o)[n]]
                    for m, t in enumerate(mine):
                        dy, dx = TAPS[t]
                        mm = pe.matmul(ps_dw[:, o, n * BANK:(n + 1) * BANK], diag[:, o, m],
                                       rows(o, k * ROWS + 1 + dy + n * BROWS, BROWS, 1 + dx),
                                       start=m == 0, stop=m == len(mine) - 1)
                mm.then_inc(dw_products, 1)

            def dw_chunk(b, k, edge=None):
                for o in range(HALVES):
                    dw_half(b, k, o, edge)

            def group_product(n, dst, src, before):
                pe.wait_ge(g_chain, after(G_STEPS, n, before))
                pe.matmul(dst, group[:], src, start=True, stop=True).then_inc(g_chain, 1)

            def x_bias(n):
                pe.wait_ge(x_chain, after(X_STEPS, n, "w1"))
                for o in range(HALVES):
                    for i in range(HALVES):
                        mm = pe.matmul(ps_b1[:, o:o + 1], w1_s[:, i, o * P:(o + 1) * P],
                                       mean[:, i:i + 1], start=i == 0, stop=i == HALVES - 1)
                mm.then_inc(x_chain, 1)

            def attention_hidden(b):
                pe.wait_ge(a_chain, after(A_STEPS, b, "pool"))
                for i in range(HALVES):
                    mm = pe.matmul(ps_hid, att1[:, i, :], pooled[:, i:i + 1],
                                   start=i == 0, stop=i == HALVES - 1)
                mm.then_inc(a_chain, 1)

            def attention_out(b):
                pe.wait_ge(a_chain, after(A_STEPS, b, "leaky"))
                for o in range(HALVES):
                    mm = pe.matmul(ps_at[:, o:o + 1], att2[:, o * P:(o + 1) * P], hidden[:],
                                   start=True, stop=True)
                mm.then_inc(a_chain, 1)

            def conv2_phase(b, last):
                conv2_weights(b)
                for k in range(3):
                    conv2_chunk(b, k)
                dw_chunk(b, 0, "first")
                conv2_chunk(b, 3)
                dw_chunk(b, 1)
                with pe.Fori(4, K - 1) as k:
                    conv2_chunk(b, k)
                    dw_chunk(b, k - 2)
                conv2_chunk(b, K - 1)
                dw_chunk(b, K - 3)
                dw_half(b, K - 2, 0)
                group_product(b + 1, ps_gm, mean[:], "var1")
                dw_half(b, K - 2, 1)
                group_product(b + 1, ps_gq, tmp4[:], "q")
                dw_half(b, K - 1, 0, "last")
                attention_hidden(b)
                dw_half(b, K - 1, 1, "last")
                attention_out(b)
                if not last:
                    x_bias(b + 1)

            pe.wait_ge(const_pool, 6)
            pe.wait_ge(const_loaded, 16 * 8)
            pe.wait_ge(const_dve, CONST_DVE)
            group_product(0, ps_gm, mean[:], "var1")
            group_product(0, ps_gq, tmp4[:], "q")
            x_bias(0)
            conv1_phase(0)
            with pe.Fori(0, B - 1) as b:
                conv2_phase(b, False)
                conv1_phase(b + 1)
            conv2_phase(B - 1, True)

        @block.scalar
        def _(act):
            def load_stat(b, k, q, wait=False):
                if wait:
                    act.wait_ge(x_summed, b * 2 * K + 2 * (k - 1))
                    act.wait_ge(x_counted, b * K + k - 1)
                act.dma_start(stat_ring[:, q], xv[:, bass.ds(b * HALVES, HALVES),
                                                  bass.ds((K - 1) * CP - k * CP, CP)]
                              ).then_inc(stat_loaded[q], 16)

            def store_out(b, k, q, o):
                act.wait_ge(out_ready, b * 2 * K + 2 * k + o + 1)
                act.dma_start(ov[:, bass.ds(b * HALVES + o, 1), bass.ds(k * CP, CP)],
                              fin_ring[:, q, o:o + 1]).then_inc(out_stored[2 * q + o], 16)

            def after_x(b, k, o):
                if o == 0:
                    act.wait_ge(x_summed, b * 2 * K + 2 * k + 2)

            def after_u(b, k, o):
                act.wait_ge(u_summed, b * 2 * K + 2 * k + o + 1)

            def after_x1(b, k, o):
                act.wait_ge(x1_squared, b * 2 * K + 2 * k + o + 1)

            def x_pivots(b):
                act.wait_ge(stat_loaded[0], 16 * (b * (K // 2) + 1))
                nc.scalar.mul(neg_pivot[:, 0:1], stat_ring[:, 0, 0, 0:1], -1.0).then_inc(x_pivot, 1)
                act.wait_ge(x_pivot, b + 1)

            def x_sum(b, j, q):
                act.wait_ge(stat_loaded[q], 16 * (b * (K // 2) + j + 1))
                src = stat_ring[:, q, 0, :]
                nc.scalar.activation(src, src, ACT.Identity, accum_out=part[:, 0, bass.ds(2 * j + q, 1)]
                                     ).then_inc(x_summed, 1)

            def x_squares(b, j, q, freed=None):
                k = 2 * j + q
                act.wait_ge(x_summed, b * 2 * K + 2 * k + 1)
                if freed is not None:
                    freed()
                nc.scalar.activation(unused[:, 2], stat_ring[:, q, 0, :], ACT.Square,
                                     bias=neg_pivot[:, 0:1],
                                     accum_out=part[:, 4, bass.ds(k, 1)]).then_inc(x_summed, 1)

            def x1_squares(b, k):
                for o in range(HALVES):
                    act.wait_ge(x1_half, b * 2 * K + 2 * k + o + 1)
                    if not (isinstance(k, int) and k == 0):
                        after_x1(b, k - 1, o)
                    nc.scalar.activation(grid(unused[:, o]), rows(o, k * ROWS + 1, ROWS), ACT.Square,
                                         bias=neg_pivot[:, 2 + o:3 + o],
                                         accum_out=part[:, 6 + o, bass.ds(k, 1)]).then_inc(x1_squared, 1)

            def u_squares(b, k, freed, skip_top=0):
                n = ROWS - skip_top
                for o in range(HALVES):
                    act.wait_ge(u_written, b * 2 * K + 2 * k + o + 1)
                    freed(o)
                    nc.scalar.activation(grid(unused[:, 2 + o])[:, 0:n, 0:W - 2],
                                         rows(o, k * ROWS + skip_top, n, 2, W - 2), ACT.Square,
                                         bias=u_neg_pivot[:, o:o + 1],
                                         accum_out=u_part[:, 2 + o, bass.ds(k, 1)]
                                         ).then_inc(u_summed, 1)

            def multiply_taps(b, k, o, numbers):
                for m in numbers:
                    dy, dx = TAPS[SUMMED_TAPS[o][m]]
                    first = isinstance(k, int) and k == 0
                    if (dy == 1 or m == 0 and first) and not (isinstance(k, int) and k == K - 1):
                        act.wait_ge(x1_half, b * 2 * K + 2 * (k + 1) + o + 1)
                    if m == 0 and not first:
                        act.wait_ge(tap_added, taps_before(b, k - 1, o) + 1)
                    if m > 1:
                        act.wait_ge(tap_summed, sums_before(b, k, o) + m - 1)
                    nc.scalar.activation(grid(tap_part[o] if m == 0 else tap_product[o]),
                                         rows(o, k * ROWS + 1 + dy, ROWS, 1 + dx), ACT.Copy,
                                         scale=taps[:, o, SUMMED_TAPS[o][m]:SUMMED_TAPS[o][m] + 1]
                                         ).then_inc(tap_multiplied, 1)

            def conv2_phase(b, last):
                def freed(k):
                    def waits(o):
                        if not last and o == 0 and (not isinstance(k, int) or k + 4 < K):
                            after_x(b + 1, k + 4, 0)
                        elif not (isinstance(k, int) and k == 0):
                            after_u(b, k - 1, o)
                    return waits

                def step(k, j, q, u_k=None, skip_top=0, freed_x=None, with_x=True):
                    with_x = with_x and not last
                    first = isinstance(k, int) and k == 0
                    load_next = not last and not (isinstance(k, int) and k + 3 >= K)
                    if first and load_next:
                        load_stat(b + 1, k + 3, 1 - q, wait=True)
                    if not (isinstance(k, int) and k < 2):
                        multiply_taps(b, k - 2, 1, range(3, summed(k - 2, 1)))
                    if not first:
                        multiply_taps(b, k - 1, 0, [0, 1])
                    x1_squares(b, k)
                    if not first:
                        multiply_taps(b, k - 1, 0, range(2, summed(k - 1, 0)))
                        multiply_taps(b, k - 1, 1, [0, 1])
                    if load_next and not first:
                        load_stat(b + 1, k + 3, 1 - q, wait=True)
                    if u_k is not None:
                        u_squares(b, u_k, freed(u_k), skip_top)
                    if not first:
                        multiply_taps(b, k - 1, 1, range(2, min(3, summed(k - 1, 1))))
                    if with_x:
                        x_sum(b + 1, j + 1, q)
                        x_squares(b + 1, j + 1, q, freed_x)

                if not last:
                    for q in range(2):
                        act.wait_ge(conv1_done, b * 2 * K + 4)
                        load_stat(b + 1, q, q)
                    x_pivots(b + 1)
                    for q in range(2):
                        x_sum(b + 1, 0, q)
                        x_squares(b + 1, 0, q, (lambda: after_x(b + 1, 0, 0)) if q else None)
                        if q == 0:
                            load_stat(b + 1, 2, 0, wait=True)
                for k in range(4):
                    step(k, k // 2, k % 2, *((0, 1) if k == 3 else ()),
                         freed_x=lambda: after_u(b, 0, 0) if k == 3 else after_x(b + 1, k + 1, 0))
                with act.Fori(2, K // 2 - 2) as j:
                    for q in range(2):
                        k = 2 * j + q
                        step(k, j, q, k - 3, freed_x=lambda: after_u(b, k - 3, 0))
                for k in range(K - 4, K):
                    step(k, k // 2, k % 2, k - 3, freed_x=lambda: after_u(b, k - 3, 0),
                         with_x=k < K - 2)
                multiply_taps(b, K - 2, 1, range(3, summed(K - 2, 1)))
                multiply_taps(b, K - 1, 0, [0, 1])
                u_squares(b, K - 3, freed(K - 3))
                multiply_taps(b, K - 1, 0, range(2, summed(K - 1, 0)))
                multiply_taps(b, K - 1, 1, [0, 1])
                u_squares(b, K - 2, freed(K - 2))
                multiply_taps(b, K - 1, 1, range(2, summed(K - 1, 1)))
                act.wait_ge(u_chain, after(U_STEPS, b, "corner"))
                after_u(b, K - 2, 1)
                for o in range(HALVES):
                    top = rows(o, 0, 1)
                    left_right = body[:, o, 1:H - ROWS, 1:W + 1:W - 1]
                    for n, (src, r, w) in enumerate(((top, 1, W), (left_right, H - ROWS - 1, 2))):
                        dst = unused[:, 2 + n, o * 2 * W:o * 2 * W + r * w]
                        made = nc.scalar.activation(dst.rearrange("p (r w) -> p r w", w=w), src,
                                                    ACT.Square, bias=u_neg_pivot[:, o:o + 1],
                                                    accum_out=u_part[:, 2 + o, K + n:K + n + 1])
                made.then_inc(edge_summed, 1)
                act.wait_ge(a_chain, after(A_STEPS, b, "att"))
                nc.scalar.activation(attn[:], ps_at, ACT.Sigmoid).then_inc(a_chain, 1)
                act.wait_ge(edge_summed, b + 1)
                for o in range(HALVES):
                    act.wait_ge(u_chain, after(U_STEPS, b, f"corner{o}"))
                    nc.scalar.activation(grid(unused[:, 2 + o]), rows(o, H - ROWS, ROWS),
                                         ACT.Square, bias=u_neg_pivot[:, o:o + 1],
                                         accum_out=u_part[:, 2 + o, K - 1:K]).then_inc(u_summed, 1)

            def relu_u(b, k, o):
                nc.scalar.activation(grid(ps_dw[:, o]), rows(o, k * ROWS, ROWS), ACT.Relu,
                                     bias=relu_shift[:, o:o + 1], scale=relu_scale[:, o:o + 1]
                                     ).then_inc(relu_done, 1)

            def write_h(b, k, o):
                act.wait_ge(conv1_done, b * 2 * K + 2 * k + o + 1)
                nc.scalar.activation(rows(o, k * ROWS + 1, ROWS), grid(ps_conv[:, o]), ACT.Relu,
                                     bias=bias1[:, o:o + 1]).then_inc(h_written, 1)

            def final_phase(b, conv1):
                def h_over_u(k):
                    for o in range(HALVES):
                        act.wait_ge(leaky_done, b * 2 * K + 2 * min_chunk(k) + o + 1)
                        write_h(b + 1, k, o)

                def min_chunk(k):
                    return k if isinstance(k, int) and k == K - 1 else k + 1

                def chunk(k, q):
                    for o in range(HALVES):
                        act.wait_ge(out_ready, b * 2 * K + 2 * k + o + 1)
                        relu_u(b, k + 1, o)
                    for o in range(HALVES):
                        store_out(b, k, q, o)
                    if conv1:
                        h_over_u(k)

                act.wait_ge(u_chain, after(U_STEPS, b, "rshift"))
                for o in range(HALVES):
                    relu_u(b, 0, o)
                with act.Fori(0, K // 2 - 1) as j:
                    for q in range(2):
                        chunk(2 * j + q, q)
                chunk(K - 2, 0)
                if conv1:
                    h_over_u(K - 1)
                else:
                    for o in range(HALVES):
                        store_out(b, K - 1, 1, o)

            act.wait_ge(const_dve, CONST_CLEARED)
            for q in range(2):
                load_stat(0, q, q)
            x_pivots(0)
            x_sum(0, 0, 0)
            x_squares(0, 0, 0)
            with act.Fori(1, K // 2) as j:
                load_stat(0, 2 * j, 0, wait=True)
                x_sum(0, j - 1, 1)
                x_squares(0, j - 1, 1, lambda: after_x(0, 2 * j - 2, 0))
                load_stat(0, 2 * j + 1, 1, wait=True)
                x_sum(0, j, 0)
                x_squares(0, j, 0, lambda: after_x(0, 2 * j - 1, 0))
            x_sum(0, K // 2 - 1, 1)
            x_squares(0, K // 2 - 1, 1, lambda: after_x(0, K - 2, 0))
            with act.Fori(0, K) as k:
                for o in range(HALVES):
                    write_h(0, k, o)
            with act.Fori(0, B - 1) as b:
                conv2_phase(b, False)
                final_phase(b, True)
            conv2_phase(B - 1, True)
            final_phase(B - 1, False)
            for n in range(4):
                act.wait_ge(out_stored[n], 16 * B * (K // 2))

        @block.vector
        def _(dve):
            V = nc.vector

            def step(chain, steps, n, name, make):
                at = steps.index(name)
                if not (at == 0):
                    dve.wait_ge(chain, n * len(steps) + at)
                make().then_inc(chain, 1)

            def g_steps_to_mean(n):
                s = lambda name, make: step(g_chain, G_STEPS, n, name, make)
                s("total", lambda: V.reduce_sum(total[:], part[:], AX_X))
                V.bn_aggr(x_mv[:], x_stats[:].rearrange("p a b -> p (a b)")).then_inc(g_chain, 1)
                s("dm", lambda: V.scalar_tensor_tensor(out=dm[:], in0=total[:, 0:4], scalar=1.0 / NPIX,
                                                       in1=neg_pivot[:], op0=ALU.mult, op1=ALU.add))
                s("dm2", lambda: V.tensor_tensor(tmp4[:], dm[:], dm[:], ALU.mult))
                s("var", lambda: V.scalar_tensor_tensor(out=var[:], in0=total[:, 4:8], scalar=1.0 / NPIX,
                                                        in1=tmp4[:], op0=ALU.mult, op1=ALU.subtract))
                s("var0", lambda: V.tensor_scalar(var[:], var[:], 0.0, None, ALU.max))
                s("mean", lambda: V.scalar_tensor_tensor(out=mean[:], in0=total[:, 0:4],
                                                         scalar=1.0 / NPIX, in1=add_back[:],
                                                         op0=ALU.mult, op1=ALU.add))
                s("mean1", lambda: V.tensor_copy(mean[:, 1:2], x_mv[:, 0:1]))
                s("var1", lambda: V.tensor_copy(var[:, 1:2], x_mv[:, 1:2]))

            def g_steps_to_q(n):
                s = lambda name, make: step(g_chain, G_STEPS, n, name, make)
                s("gmean", lambda: V.tensor_copy(gmean[:], ps_gm))
                s("dev", lambda: V.tensor_tensor(dev[:], mean[:], gmean[:], ALU.subtract))
                s("dev2", lambda: V.tensor_tensor(tmp4[:], dev[:], dev[:], ALU.mult))
                s("q", lambda: V.tensor_tensor(tmp4[:], tmp4[:], var[:], ALU.add))

            def g_steps_to_ve(n):
                step(g_chain, G_STEPS, n, "ve", lambda: V.tensor_scalar(tmp4[:], ps_gq, EPS, None, ALU.add))

            def x_steps_to_weights(n):
                s = lambda name, make: step(x_chain, X_STEPS, n, name, make)
                dve.wait_ge(g_chain, after(G_STEPS, n, "rstd"))
                s("t", lambda: V.tensor_tensor(xs_[:], var[:, 0:2], grstd[:, 0:2], ALU.mult))
                s("t2", lambda: V.tensor_tensor(xs_[:], xs_[:], grstd[:, 0:2], ALU.mult))
                s("te", lambda: V.tensor_scalar(xs_[:], xs_[:], EPS, None, ALU.add))
                dve.wait_ge(x_chain, after(X_STEPS, n, "rstd"))
                V.tensor_tensor(xs_[:], xr[:], grstd[:, 0:2], ALU.mult).then_inc(x_chain, 1)
                for i in range(HALVES):
                    s(f"w{i}", lambda i=i: V.tensor_scalar(w1_s[:, i, :], w1_raw[:, i, :],
                                                           xs_[:, i:i + 1], None, ALU.mult))

            def x_steps_to_bias(n):
                s = lambda name, make: step(x_chain, X_STEPS, n, name, make)
                s("bias", lambda: V.tensor_tensor(bias1[:], b1c, ps_b1, ALU.subtract))
                s("pivots", lambda: V.tensor_scalar(neg_pivot[:, 2:4], mean[:, 0:2], -1.0, None, ALU.mult))

            def u_pivot_step(n):
                s = lambda name, make: step(x_chain, X_STEPS, n, name, make)
                s("upivot", lambda: V.tensor_tensor(u_neg_pivot[:], neg_pivot[:, 2:4], tap_sum[:], ALU.mult))

            def h_steps(b):
                s = lambda name, make: step(h_chain, H_STEPS, b, name, make)
                dve.wait_ge(h_counted, (b + 1) * 2 * K)
                s("top", lambda: V.memset(body[:, :, 0, :], 0.0))
                for i in range(HALVES):
                    V.bn_aggr(h_mv[:, i, :], h_stats[:, i].rearrange("p a b -> p (a b)")
                              ).then_inc(h_chain, 1)
                s("ve", lambda: V.tensor_scalar(h_ve[:], h_mv[:, :, 1], EPS, None, ALU.add))
                for i in range(HALVES):
                    s(f"w{i}", lambda i=i: V.tensor_scalar(w2_s[:, i, :], w2_raw[:, i, :],
                                                           h_rstd[:, i:i + 1], None, ALU.mult))
                s("neg", lambda: V.tensor_tensor(neg_beta2[:], ps_b2, b2c, ALU.subtract))
                s("beta", lambda: V.tensor_scalar(beta2[:], neg_beta2[:], -1.0, None, ALU.mult))

            def back_step(b):
                step(h_chain, H_STEPS, b, "back", lambda: V.tensor_copy(add_back[:, 2:4], beta2[:]))

            def x1_writers(b, j, q):
                k = 2 * j + q
                ps = ps_dw if isinstance(k, int) and k == 1 else ps_conv

                def half(o):
                    if o == 0:
                        dve.wait_ge(conv2_done, b * K + k + 1)
                        dve.wait_ge(x_loaded[q], 16 * (b * (K - 1) + K // 2 + j))
                    V.scalar_tensor_tensor(out=rows(o, k * ROWS + 1, ROWS), in0=grid(ps[:, o]),
                                           scalar=neg_beta2[:, o:o + 1], in1=grid(x_ring[:, q, o]),
                                           op0=ALU.max, op1=ALU.add,
                                           accum_out=part[:, 2 + o, bass.ds(k, 1)]).then_inc(x1_half, 1)

                return [lambda: half(0), lambda: half(1)]

            def write_x1(b, j, q):
                for write in x1_writers(b, j, q):
                    write()

            def x_counters(b, j, q):
                def bank(n):
                    if n == 0:
                        dve.wait_ge(stat_loaded[q], 16 * (b * (K // 2) + j + 1))
                    ins = V.bn_stats(x_stats[:, bass.ds(4 * j + 2 * q + n, 1), :].rearrange("p a b -> p (a b)"),
                                     stat_ring[:, q, 1, n * BANK:(n + 1) * BANK])
                    if n == 1:
                        ins.then_inc(x_counted, 1)

                return [lambda: bank(0), lambda: bank(1)]

            def count_x(b, j, q):
                for count in x_counters(b, j, q):
                    count()

            def write_u(b, k, j, q, o, between=()):
                between = list(between)
                dve.wait_ge(dw_products, b * 2 * K + 2 * k + o + 1)
                dve.wait_ge(tap_summed, sums_before(b, k, o) + summed(k, o) - 1)
                V.tensor_tensor(ps_dw[:, o], ps_dw[:, o], tap_part[o], ALU.add).then_inc(tap_added, 1)
                mine = vector_taps(o, division(k, o), summed(k, o))
                for m, (t, bank) in enumerate(mine):
                    dy, dx = TAPS[t]
                    if m == len(mine) - 1:
                        dve.wait_ge(x1_squared, b * 2 * K + 2 * k + o + 1)
                        dve.wait_ge(spilled[q], 32 * (b * (K // 2) + j + 1))
                    if between:
                        between.pop(0)()
                    dve.wait_ge(tap_added, taps_before(b, k, o) + m + 1)
                    if m == len(mine) - 1:
                        V.scalar_tensor_tensor(out=rows(o, k * ROWS, ROWS),
                                               in0=rows(o, k * ROWS + 1 + dy, ROWS, 1 + dx),
                                               scalar=taps[:, o, t:t + 1], in1=grid(ps_dw[:, o]),
                                               op0=ALU.mult, op1=ALU.add,
                                               accum_out=u_part[:, o, bass.ds(k, 1)]
                                               ).then_inc(u_written, 1)
                    else:
                        top, n = (0, ROWS) if bank is None else (bank * BROWS, BROWS)
                        sums = grid(ps_dw[:, o, top * W:(top + n) * W])
                        V.scalar_tensor_tensor(out=sums, in0=rows(o, k * ROWS + 1 + dy + top, n, 1 + dx),
                                               scalar=taps[:, o, t:t + 1], in1=sums,
                                               op0=ALU.mult, op1=ALU.add).then_inc(tap_added, 1)
                assert not between

            def hidden_steps(b):
                s = lambda name, make: step(a_chain, A_STEPS, b, name, make)
                s("copy", lambda: V.tensor_copy(hidden_raw[:], ps_hid))
                s("leaky", lambda: V.scalar_tensor_tensor(out=hidden[:], in0=hidden_raw[:], scalar=SLOPE,
                                                          in1=hidden_raw[:], op0=ALU.mult, op1=ALU.max))

            def k_steps(b):
                s = lambda name, make: step(k_chain, K_STEPS, b, name, make)
                s("k", lambda: V.tensor_tensor(padk[:], gmean[:, 2:4], beta2[:], ALU.subtract))
                wide = padk[:].unsqueeze(2).to_broadcast([P, HALVES, 2])
                s("krows", lambda: V.tensor_tensor(k_rows[:], edge_rows[:], wide, ALU.mult))
                s("kcols", lambda: V.tensor_tensor(k_cols[:], edge_cols[:], wide, ALU.mult))
                corners = taps[:].rearrange("p o (y x) -> p o y x", x=3)[:, :, 0:3:2, 0:3:2]
                s("kcorner", lambda: V.tensor_tensor(
                    k_corner[:], corners,
                    padk[:].unsqueeze(2).unsqueeze(3).to_broadcast([P, HALVES, 2, 2]), ALU.mult))
                s("ksum", lambda: V.tensor_tensor(u_part[:, 0:2, K], padk[:], edge_weight[:], ALU.mult))
                s("kpivot", lambda: V.tensor_scalar(u_part[:, 0:2, K + 1], u_neg_pivot[:],
                                                    float(NPIX), None, ALU.mult))
                s("kw", lambda: V.tensor_tensor(v(5), padk[:], tap_sum[:], ALU.mult))

            def a_steps_to_end(b):
                s = lambda name, make: step(a_chain, A_STEPS, b, name, make)
                s("alpha", lambda: V.tensor_tensor(alpha[:], attn[:], grstd[:, 2:4], ALU.mult))
                s("akw", lambda: V.tensor_tensor(v(5), v(5), alpha[:], ALU.mult))
                s("c0", lambda: V.tensor_tensor(v(5), rbc, v(5), ALU.subtract))

            def v(i):
                return uv[:, i, :]

            def edge_steps(b):
                s = lambda name, make: step(u_chain, U_STEPS, b, name, make)
                dve.wait_ge(k_chain, after(K_STEPS, b, "kw"))
                dve.wait_ge(u_summed, b * 2 * K + 2 * (K - 1))
                t = body[:, :, 0, 1:W + 1]
                s("top", lambda: V.tensor_tensor(t, t, k_rows[:, :, 0:1].to_broadcast([P, HALVES, W]), ALU.add))
                n = H - ROWS
                lr = body[:, :, 0:n, 1:W + 1:W - 1]
                s("cols", lambda: V.tensor_tensor(lr, lr, k_cols[:].unsqueeze(2).to_broadcast([P, HALVES, n, 2]), ALU.add))
                c = body[:, :, 0, 1:W + 1:W - 1]
                s("corner", lambda: V.tensor_tensor(c, c, k_corner[:, :, 0, :], ALU.subtract))

            def last_edge_steps(b, o):
                s = lambda name, make: step(u_chain, U_STEPS, b, name, make)
                r = body[:, o, H - 1, 1:W + 1]
                dve.wait_ge(u_written, b * 2 * K + 2 * (K - 1) + o + 1)
                s(f"bottom{o}", lambda: V.tensor_scalar(r, r, k_rows[:, o, 1:2], None, ALU.add))
                lr = body[:, o, H - ROWS:H, 1:W + 1:W - 1]
                s(f"cols{o}", lambda: V.tensor_tensor(lr, lr, k_cols[:, o:o + 1, :].to_broadcast([P, ROWS, 2]), ALU.add))
                c = body[:, o, H - 1, 1:W + 1:W - 1]
                s(f"corner{o}", lambda: V.tensor_tensor(c, c, k_corner[:, o, 1, :], ALU.subtract))

            def u_steps(b):
                s = lambda name, make: step(u_chain, U_STEPS, b, name, make)
                side = lambda name, make: step(m_chain, M_STEPS, b, name, make)
                dve.wait_ge(u_summed, (b + 1) * 2 * K)
                dve.wait_ge(a_chain, after(A_STEPS, b, "c0"))
                s("total", lambda: V.reduce_sum(u_total[:], u_part[:], AX_X))
                s("m", lambda: V.tensor_scalar(v(0), u_total[:, 0:2], 1.0 / NPIX, None, ALU.mult))
                s("m2", lambda: V.tensor_tensor(v(1), v(0), v(0), ALU.mult))
                s("var", lambda: V.scalar_tensor_tensor(out=v(1), in0=u_total[:, 2:4], scalar=1.0 / NPIX,
                                                        in1=v(1), op0=ALU.mult, op1=ALU.subtract))
                s("vt", lambda: V.scalar_tensor_tensor(out=v(3), in0=v(1), scalar=0.0, in1=alpha[:],
                                                       op0=ALU.max, op1=ALU.mult))
                s("vt2", lambda: V.tensor_tensor(v(3), v(3), alpha[:], ALU.mult))
                s("te", lambda: V.tensor_scalar(v(3), v(3), EPS, None, ALU.add))
                side("mean", lambda: V.tensor_tensor(v(0), v(0), u_neg_pivot[:], ALU.subtract))
                side("am", lambda: V.tensor_tensor(v(6), alpha[:], v(0), ALU.mult))
                side("mu", lambda: V.tensor_tensor(v(6), v(6), v(5), ALU.add))
                side("d", lambda: V.tensor_tensor(v(7), v(5), v(6), ALU.subtract))
                dve.wait_ge(m_chain, after(M_STEPS, b, "d"))
                s("rscale", lambda: V.scalar_tensor_tensor(out=relu_scale[:], in0=alpha[:], scalar=1.0 - SLOPE,
                                                           in1=v(4), op0=ALU.mult, op1=ALU.mult))
                s("rshift", lambda: V.scalar_tensor_tensor(out=relu_shift[:], in0=v(7), scalar=1.0 - SLOPE,
                                                           in1=v(4), op0=ALU.mult, op1=ALU.mult))
                s("sscale", lambda: V.scalar_tensor_tensor(out=slope_scale[:], in0=alpha[:], scalar=SLOPE,
                                                           in1=v(4), op0=ALU.mult, op1=ALU.mult))
                s("oshift", lambda: V.scalar_tensor_tensor(out=v(2), in0=v(7), scalar=SLOPE,
                                                           in1=v(4), op0=ALU.mult, op1=ALU.mult))
                s("last", lambda: V.tensor_tensor(out_shift[:], v(2), beta2[:], ALU.add))

            def conv2_phase(b, last):
                def write_both(j, q, k_u, j_u, with_x=True):
                    write_u(b, k_u, j_u, q, 0, x1_writers(b, j, q))
                    write_u(b, k_u, j_u, q, 1, x_counters(b + 1, j + 1, q) if with_x and not last else ())

                if not last:
                    count_x(b + 1, 0, 0)
                    count_x(b + 1, 0, 1)
                write_x1(b, 0, 0)
                if not last:
                    count_x(b + 1, 1, 0)
                write_x1(b, 0, 1)
                if not last:
                    count_x(b + 1, 1, 1)
                write_x1(b, 1, 0)
                write_u(b, 0, 0, 0, 0)
                write_u(b, 0, 0, 0, 1, x_counters(b + 1, 2, 0) if not last else ())
                write_x1(b, 1, 1)
                write_u(b, 1, 0, 1, 0)
                write_u(b, 1, 0, 1, 1, x_counters(b + 1, 2, 1) if not last else ())
                with dve.Fori(2, K // 2 - 1) as j:
                    for q in range(2):
                        write_both(j, q, 2 * j + q - 2, j - 1)
                for q in range(2):
                    write_both(K // 2 - 1, q, K - 4 + q, K // 2 - 2, with_x=False)
                dve.wait_ge(x1_squared, (b + 1) * 2 * K)
                dve.wait_ge(x_summed, (b + 2) * 2 * K if not last else B * 2 * K)
                dve.wait_ge(x_counted, (b + 2) * K if not last else B * K)
                g_steps_to_mean(b + 1)
                write_u(b, K - 2, K // 2 - 1, 0, 0)
                g_steps_to_q(b + 1)
                k_steps(b)
                g_steps_to_ve(b + 1)
                write_u(b, K - 2, K // 2 - 1, 0, 1)
                dve.wait_ge(g_chain, after(G_STEPS, b + 1, "rstd"))
                step(a_chain, A_STEPS, b, "pool",
                     lambda: V.tensor_tensor(pooled[:], dev[:, 2:4], grstd[:, 2:4], ALU.mult))
                if not last:
                    x_steps_to_weights(b + 1)
                edge_steps(b)
                write_u(b, K - 1, K // 2 - 1, 1, 0)
                hidden_steps(b)
                last_edge_steps(b, 0)
                write_u(b, K - 1, K // 2 - 1, 1, 1)
                last_edge_steps(b, 1)
                if not last:
                    x_steps_to_bias(b + 1)
                a_steps_to_end(b)
                u_steps(b)
                if not last:
                    u_pivot_step(b + 1)

            def add_slope(b, j, q):
                at = b * 2 * K + 4 * j + 2 * q
                for o in range(HALVES):
                    dve.wait_ge(relu_done, at + o + 1)
                    V.scalar_tensor_tensor(out=grid(ps_dw[:, o]), in0=rows(o, (2 * j + q) * ROWS, ROWS),
                                           scalar=slope_scale[:, o:o + 1], in1=grid(ps_dw[:, o]),
                                           op0=ALU.mult, op1=ALU.add).then_inc(leaky_done, 1)

            def add_x1(b, j, q):
                at = b * 2 * K + 4 * j + 2 * q
                for o in range(HALVES):
                    dve.wait_ge(fin_loaded[2 * q + o], 16 * (b * (K // 2) + j + 1))
                    dve.wait_ge(leaky_done, at + o + 1)
                    V.scalar_tensor_tensor(out=fin_ring[:, q, o], in0=ps_dw[:, o],
                                           scalar=out_shift[:, o:o + 1], in1=fin_ring[:, q, o],
                                           op0=ALU.add, op1=ALU.add).then_inc(out_ready, 1)

            def make_out(b, j, q):
                add_slope(b, j, q)
                add_x1(b, j, q)

            def count_h(b, j, q):
                for o in range(HALVES):
                    dve.wait_ge(h_written, b * 2 * K + 4 * j + 2 * q + o + 1)
                    for n in range(2):
                        k2 = 4 * j + 2 * q + n
                        ins = V.bn_stats(h_stats[:, o, bass.ds(k2, 1), :].rearrange("p a b -> p (a b)"),
                                         rows(o, 2 * (2 * j + q) * BROWS + 1 + n * BROWS, BROWS))
                    ins.then_inc(h_counted, 1)

            V.memset(part[:], 0.0).then_inc(const_dve, 1)
            V.memset(neg_pivot[:], 0.0).then_inc(const_dve, 1)
            V.memset(add_back[:], 0.0).then_inc(const_dve, 1)
            for pads in (body[:, :, 0:H + 2:H + 1, :], body[:, :, 1:H + 1, 0:W + 2:W + 1]):
                V.memset(pads, 0.0).then_inc(const_dve, 1)
            with dve.Fori(0, K // 2) as j:
                for q in range(2):
                    count_x(0, j, q)
            dve.wait_ge(const_loaded, 16 * 8)
            dve.wait_ge(const_pool, 6)
            for o in range(HALVES):
                for m, t in enumerate(OTHER_TAPS[o][:MOST_TENSOR_TAPS]):
                    V.tensor_scalar(diag[:, o, m, :], ident[:], taps[:, o, t:t + 1], None, ALU.mult
                                    ).then_inc(const_dve, 1)
            V.reduce_sum(edge_rows[:], taps[:].rearrange("p o (y x) -> p o y x", x=3)[:, :, 0:3:2, :],
                         AX_X).then_inc(const_dve, 1)
            V.reduce_sum(edge_cols[:], taps[:].rearrange("p o (y x) -> p o x y", x=3)[:, :, 0:3:2, :],
                         AX_X).then_inc(const_dve, 1)
            V.reduce_sum(tap_sum[:], taps[:], AX_X).then_inc(const_dve, 1)
            for o in range(HALVES):
                V.reduce_sum(corner_sum[:, o:o + 1],
                             taps[:, o].rearrange("p (y x) -> p y x", x=3)[:, 0:3:2, 0:3:2],
                             mybir.AxisListType.XY).then_inc(const_dve, 1)
            dve.wait_ge(const_dve, CONST_DVE - 1)
            V.tensor_tensor(edge_weight[:], edge_rows[:, :, 0], edge_rows[:, :, 1], ALU.add).then_inc(const_dve, 1)
            for i in range(2):
                dve.wait_ge(const_dve, CONST_DVE + i)
                V.tensor_tensor(edge_weight[:], edge_weight[:], edge_cols[:, :, i], ALU.add).then_inc(const_dve, 1)
            dve.wait_ge(const_dve, CONST_DVE + 2)
            V.scalar_tensor_tensor(out=edge_weight[:], in0=edge_weight[:], scalar=float(W), in1=corner_sum[:],
                                   op0=ALU.mult, op1=ALU.subtract).then_inc(const_dve, 1)

            dve.wait_ge(const_dve, CONST_DVE + 3)
            dve.wait_ge(x_summed, 2 * K)
            dve.wait_ge(x_counted, K)
            g_steps_to_mean(0)
            g_steps_to_q(0)
            g_steps_to_ve(0)
            x_steps_to_weights(0)
            x_steps_to_bias(0)
            u_pivot_step(0)
            with dve.Fori(0, K // 2) as j:
                for q in range(2):
                    count_h(0, j, q)
            h_steps(0)
            back_step(0)
            with dve.Fori(0, B - 1) as b:
                conv2_phase(b, False)
                make_out(b, 0, 0)
                make_out(b, 0, 1)
                count_h(b + 1, 0, 0)
                with dve.Fori(1, K // 2 - 1) as j:
                    for q in range(2):
                        make_out(b, j, q)
                        count_h(b + 1, j - 1 + q, 1 - q)
                j = K // 2 - 1
                make_out(b, j, 0)
                count_h(b + 1, j - 1, 1)
                add_slope(b, j, 1)
                count_h(b + 1, j, 0)
                add_x1(b, j, 1)
                count_h(b + 1, j, 1)
                h_steps(b + 1)
                dve.wait_ge(out_ready, (b + 1) * 2 * K)
                back_step(b + 1)
            conv2_phase(B - 1, True)
            with dve.Fori(0, K // 2) as j:
                for q in range(2):
                    make_out(B - 1, j, q)


def kernel(**inputs):
    import numpy as np
    import concourse.bacc as bacc
    from concourse.bass_utils import run_bass_kernel_spmd

    C = inputs["x"].shape[1]
    column = lambda a: np.ascontiguousarray(np.asarray(a).reshape(2, C // 2).T)
    arrays = {
        "x": np.ascontiguousarray(inputs["x"]),
        "w1t": np.ascontiguousarray(np.asarray(inputs["L0_conv_w1"]).T),
        "b1": column(inputs["L0_conv_b1"]),
        "w2t": np.ascontiguousarray(np.asarray(inputs["L0_conv_w2"]).T),
        "b2": column(inputs["L0_conv_b2"]),
        "a1t": np.ascontiguousarray(np.asarray(inputs["L1_conv_attn_w1"]).T),
        "a2t": np.ascontiguousarray(np.asarray(inputs["L1_conv_attn_w2"]).T),
        "rw": np.ascontiguousarray(np.asarray(inputs["L1_conv_refine_w"]).reshape(C, 9)),
        "rb": column(inputs["L1_conv_refine_b"]),
    }
    nc = bacc.Bacc("TRN2", target_bir_lowering=False, num_devices=1)
    aps = [nc.dram_tensor(f"in_{n}", a.shape, mybir.dt.from_np(a.dtype), kind="ExternalInput").ap()
           for n, a in arrays.items()]
    out = nc.dram_tensor("out_0", inputs["x"].shape, F32, kind="ExternalOutput").ap()
    conv_preact_kernel(nc, *aps, out)
    r = run_bass_kernel_spmd(nc, [{f"in_{n}": a for n, a in arrays.items()}], core_ids=[0])
    return r.results[0]["out_0"]
```
